# Optimizing a Trainium2 kernel written in Bass

```python
import numpy as np
import jax
import jax.numpy as jnp

def _softmax(x, axis=-1):
    return jax.nn.softmax(x, axis=axis)

def _gelu(x):
    return jax.nn.gelu(x, approximate=True)

def _silu(x):
    return jax.nn.silu(x)

def _sigmoid(x):
    return jax.nn.sigmoid(x)

def _layernorm(x, axis=-1, eps=1e-05):
    m = jnp.mean(x, axis=axis, keepdims=True)
    v = jnp.var(x, axis=axis, keepdims=True)
    return (x - m) / jnp.sqrt(v + eps)

def _scatter_add(tgt, idx, src, axis=0):
    return tgt.at[idx].add(src)

def _segment_sum(src, seg, n):
    return jax.ops.segment_sum(src, seg, n)
kernel_name = 'mk_xattn_seq_d2_seqx_r4_70867c'

def setup_inputs(seed: int=0):
    np.random.seed(seed)
    _w = jnp.asarray

    def _rec_inputs():
        import jax
        import jax.numpy as jnp
        _rk = jax.random.key(seed)
        x = -0.000296 + 1 * jax.random.normal(jax.random.fold_in(_rk, 1), (16, 256, 320), jnp.float32)
        _lenS = 256 - jax.random.randint(jax.random.fold_in(_rk, 7), (16,), 0, max(1, 256 // 4) + 1, jnp.int32)
        _lenS2 = 256 - jax.random.randint(jax.random.fold_in(_rk, 8), (16,), 0, max(1, 256 // 4) + 1, jnp.int32)
        _ctx_2048P = jax.random.normal(jax.random.fold_in(_rk, 11), (16, 16, 512), jnp.float32)
        _ctx_2048c = jax.random.dirichlet(jax.random.fold_in(_rk, 511), 0.3 * jnp.ones((16,), jnp.float32), (16, 256))
        _ctx_2048t = jnp.einsum('bsk,bkd->bsd', _ctx_2048c, _ctx_2048P)
        _ctx_2048t = _ctx_2048t * jax.lax.rsqrt(jnp.mean(jnp.square(_ctx_2048t)) + 1e-12) * 0.953939
        ctx_2048 = 0.00100794 + 0.99956 * (_ctx_2048t + 0.3 * jax.random.normal(jax.random.fold_in(_rk, 611), (16, 256, 512), jnp.float32))
        fside_S_0 = jax.random.uniform(jax.random.fold_in(_rk, 12), (256,), jnp.float32, 0.0, 0.999707)
        return (x, ctx_2048, fside_S_0)
    x, ctx_2048, fside_S_0 = _rec_inputs()

    def _L0_xattn_setup():
        import jax, jax.numpy as jnp
        import numpy as np
        import math
        HEADS = 20
        NUM_TOKENS = 4
        SEM_SCALE = 0.5
        IP_SCALE = 1.0
        TEXT_LEN = 77

        def _split_heads(x, B, H, D):
            return x.reshape(B, -1, H, D).transpose(0, 2, 1, 3)
        key = jax.random.key(seed)
        ks = jax.random.split(key, 10)
        B, S, C, CD = (4, 1024, 320, 512)

        def g(k, shape, std=1.0):
            return jax.random.normal(k, shape, dtype=jnp.float32) * std
        return {'hidden_states': g(ks[0], (B, S, C)), 'encoder_hidden_states': g(ks[1], (B, TEXT_LEN + NUM_TOKENS, CD)), 'spatial_mask': jax.random.uniform(ks[2], (S,), dtype=jnp.float32), 'Wq': g(ks[3], (C, C), 1.0 / math.sqrt(C)), 'Wk': g(ks[4], (CD, C), 1.0 / math.sqrt(CD)), 'Wv': g(ks[5], (CD, C), 1.0 / math.sqrt(CD)), 'Wk_ip': g(ks[6], (CD, C), 1.0 / math.sqrt(CD)), 'Wv_ip': g(ks[7], (CD, C), 1.0 / math.sqrt(CD)), 'Wout': g(ks[8], (C, C), 1.0 / math.sqrt(C)), 'bout': jnp.zeros((C,), dtype=jnp.float32)}
    _L0_xattn_all = _L0_xattn_setup()
    _L0_xattn_in = {k: v for k, v in _L0_xattn_all.items() if k in ('Wq', 'Wk', 'Wv', 'Wk_ip', 'Wv_ip', 'Wout', 'bout')}
    del _L0_xattn_all

    def _L1_xattn_setup():
        import jax, jax.numpy as jnp
        import numpy as np
        HEADS = 20
        NUM_TOKENS = 4
        IP_SCALE = 1.0
        SEM_SCALE = 0.5
        RESCALE = 1.0
        EPS = 1e-12

        def _l2norm(x, axis=-1):
            n = jnp.sqrt(jnp.sum(x * x, axis=axis, keepdims=True))
            return x / jnp.maximum(n, EPS)
        key = jax.random.key(seed)
        ks = jax.random.split(key, 10)
        B, S, C = (2, 256, 320)
        T, E = (81, 512)
        inp = {'hidden_states': jax.random.normal(ks[0], (B, S, C), jnp.float32), 'encoder_hidden_states': jax.random.normal(ks[1], (B, T, E), jnp.float32), 'spatial_mask': jax.random.uniform(ks[2], (S,), jnp.float32), 'W_q': jax.random.normal(ks[3], (C, C), jnp.float32) * C ** (-0.5), 'W_k': jax.random.normal(ks[4], (E, C), jnp.float32) * E ** (-0.5), 'W_v': jax.random.normal(ks[5], (E, C), jnp.float32) * E ** (-0.5), 'W_k_ip': jax.random.normal(ks[6], (E, C), jnp.float32) * E ** (-0.5), 'W_v_ip': jax.random.normal(ks[7], (E, C), jnp.float32) * E ** (-0.5), 'W_out': jax.random.normal(ks[8], (C, C), jnp.float32) * C ** (-0.5), 'b_out': jnp.zeros((C,), jnp.float32)}
        return inp
    _L1_xattn_all = _L1_xattn_setup()
    _L1_xattn_in = {k: v for k, v in _L1_xattn_all.items() if k in ('W_q', 'W_k', 'W_v', 'W_k_ip', 'W_v_ip', 'W_out', 'b_out')}
    del _L1_xattn_all
    return {'x': x, 'ctx_2048': ctx_2048, 'fside_S_0': fside_S_0, 'L0_xattn_Wq': _L0_xattn_in['Wq'], 'L0_xattn_Wk': _L0_xattn_in['Wk'], 'L0_xattn_Wv': _L0_xattn_in['Wv'], 'L0_xattn_Wk_ip': _L0_xattn_in['Wk_ip'], 'L0_xattn_Wv_ip': _L0_xattn_in['Wv_ip'], 'L0_xattn_Wout': _L0_xattn_in['Wout'], 'L0_xattn_bout': _L0_xattn_in['bout'], 'L1_xattn_W_q': _L1_xattn_in['W_q'], 'L1_xattn_W_k': _L1_xattn_in['W_k'], 'L1_xattn_W_v': _L1_xattn_in['W_v'], 'L1_xattn_W_k_ip': _L1_xattn_in['W_k_ip'], 'L1_xattn_W_v_ip': _L1_xattn_in['W_v_ip'], 'L1_xattn_W_out': _L1_xattn_in['W_out'], 'L1_xattn_b_out': _L1_xattn_in['b_out']}

def reference(x, ctx_2048, fside_S_0, L0_xattn_Wq, L0_xattn_Wk, L0_xattn_Wv, L0_xattn_Wk_ip, L0_xattn_Wv_ip, L0_xattn_Wout, L0_xattn_bout, L1_xattn_W_q, L1_xattn_W_k, L1_xattn_W_v, L1_xattn_W_k_ip, L1_xattn_W_v_ip, L1_xattn_W_out, L1_xattn_b_out):
    import jax
    import jax.numpy as jnp

    def _L0_xattn_ref(hidden_states, encoder_hidden_states, spatial_mask, Wq, Wk, Wv, Wk_ip, Wv_ip, Wout, bout):
        import jax, jax.numpy as jnp
        import numpy as np
        import math
        HEADS = 20
        NUM_TOKENS = 4
        SEM_SCALE = 0.5
        IP_SCALE = 1.0
        TEXT_LEN = 77

        def _split_heads(x, B, H, D):
            return x.reshape(B, -1, H, D).transpose(0, 2, 1, 3)
        B, S, C = hidden_states.shape
        D = C // HEADS
        scale = 1.0 / math.sqrt(D)
        residual = hidden_states
        text = encoder_hidden_states[:, :TEXT_LEN]
        ip = encoder_hidden_states[:, TEXT_LEN:]
        q = hidden_states @ Wq
        k_text = text @ Wk
        v_text = text @ Wv
        q_h = _split_heads(q, B, HEADS, D)
        k_h = _split_heads(k_text, B, HEADS, D)
        v_h = _split_heads(v_text, B, HEADS, D)
        logits = jnp.einsum('bhqd,bhkd->bhqk', q_h, k_h) * scale
        probs = jax.nn.softmax(logits, axis=-1)
        text_out = jnp.einsum('bhqk,bhkd->bhqd', probs, v_h)
        text_out = text_out.transpose(0, 2, 1, 3).reshape(B, S, C)
        ip_k = ip @ Wk_ip
        ip_v = ip @ Wv_ip
        ip_k_h = _split_heads(ip_k, B, HEADS, D)
        ip_v_h = _split_heads(ip_v, B, HEADS, D)
        scores = jnp.einsum('bhqd,bhkd->bhqk', q_h, ip_k_h) * scale
        text_probs = jax.nn.softmax(jnp.einsum('bqc,bkc->bqk', q, k_text) * scale, axis=-1)
        q_sem = jnp.einsum('bqk,bkc->bqc', text_probs, text)
        sem = jnp.einsum('bqc,bnc->bqn', q_sem, ip) * scale
        sem = jax.lax.stop_gradient(sem)
        fused = scores + SEM_SCALE * sem[:, None, :, :]
        ip_probs = jax.nn.softmax(fused, axis=-1)
        ip_probs = ip_probs * spatial_mask[None, None, :, None]
        ip_out = jnp.einsum('bhqk,bhkd->bhqd', ip_probs, ip_v_h)
        ip_out = ip_out.transpose(0, 2, 1, 3).reshape(B, S, C)
        hs = text_out + IP_SCALE * ip_out
        out = hs @ Wout + bout
        out = out + residual
        return out

    def _L1_xattn_ref(hidden_states, encoder_hidden_states, spatial_mask, W_q, W_k, W_v, W_k_ip, W_v_ip, W_out, b_out):
        import jax, jax.numpy as jnp
        import numpy as np
        HEADS = 20
        NUM_TOKENS = 4
        IP_SCALE = 1.0
        SEM_SCALE = 0.5
        RESCALE = 1.0
        EPS = 1e-12

        def _l2norm(x, axis=-1):
            n = jnp.sqrt(jnp.sum(x * x, axis=axis, keepdims=True))
            return x / jnp.maximum(n, EPS)
        B, S, C = hidden_states.shape
        H = HEADS
        Dh = C // H
        attn_scale = Dh ** (-0.5)
        residual = hidden_states
        text_ehs = encoder_hidden_states[:, :-NUM_TOKENS]
        ip_ehs = encoder_hidden_states[:, -NUM_TOKENS:]

        def heads(x):
            return x.reshape(B, -1, H, Dh).transpose(0, 2, 1, 3)
        q = heads(hidden_states @ W_q)
        k_t = heads(text_ehs @ W_k)
        v_t = heads(text_ehs @ W_v)
        scores_t = jnp.einsum('bhsd,bhtd->bhst', q, k_t) * attn_scale
        probs_t = jax.nn.softmax(scores_t, axis=-1)
        text_out = jnp.einsum('bhst,bhtd->bhsd', probs_t, v_t)
        text_out = text_out.transpose(0, 2, 1, 3).reshape(B, S, C)
        k_ip = heads(ip_ehs @ W_k_ip)
        v_ip = heads(ip_ehs @ W_v_ip)
        attn_scores = jnp.einsum('bhsd,bhnd->bhsn', q, k_ip) * attn_scale
        qsem = jnp.einsum('bhst,bte->bhse', probs_t, text_ehs)
        qsem = _l2norm(qsem)
        ip_n = _l2norm(ip_ehs)
        sem = jnp.einsum('bhse,bne->bhsn', qsem, ip_n)
        sem = jax.lax.stop_gradient(sem)
        fused = attn_scores + SEM_SCALE * sem
        probs_ip = jax.nn.softmax(fused, axis=-1)
        probs_ip = probs_ip * spatial_mask[None, None, :, None]
        ip_out = jnp.einsum('bhsn,bhnd->bhsd', probs_ip, v_ip)
        ip_out = ip_out.transpose(0, 2, 1, 3).reshape(B, S, C)
        out = text_out + IP_SCALE * ip_out
        out = out @ W_out + b_out
        out = out + residual
        return out / RESCALE
    x = _L0_xattn_ref(x, ctx_2048, fside_S_0, L0_xattn_Wq, L0_xattn_Wk, L0_xattn_Wv, L0_xattn_Wk_ip, L0_xattn_Wv_ip, L0_xattn_Wout, L0_xattn_bout)
    x = _L1_xattn_ref(x, ctx_2048, fside_S_0, L1_xattn_W_q, L1_xattn_W_k, L1_xattn_W_v, L1_xattn_W_k_ip, L1_xattn_W_v_ip, L1_xattn_W_out, L1_xattn_b_out)
    return x

_drawn_inputs = setup_inputs


def setup_inputs(seed=0):
    import zlib

    import numpy as np

    out = dict(_drawn_inputs(seed))
    spreads = {'L0_xattn_bout': (0.0, 0.1), 'L1_xattn_b_out': (0.0, 0.1)}
    factors = {}
    for name, (base, spread) in spreads.items():
        noise = np.random.default_rng([zlib.crc32(name.encode()), seed]).standard_normal(out[name].shape)
        drawn = base * np.exp(spread * noise) if base else spread * noise
        out[name] = jnp.asarray(drawn.astype(out[name].dtype))
    for name, factor in factors.items():
        out[name] = (out[name] * factor).astype(out[name].dtype)
    return out
```

```python
from contextlib import ExitStack

import concourse.bass as bass
from concourse import mybir

F32 = mybir.dt.float32
BF16 = mybir.dt.bfloat16
ALU = mybir.AluOpType
ACT = mybir.ActivationFunctionType
AX = mybir.AxisListType

B, S, C, CD, H, D = 16, 256, 320, 512, 20, 16
T = 256
HG = 4
SLOT = 32
CC = [(0, 107), (107, 107), (214, 106)]
MT = [(0, 128), (128, 128), (256, 64)]
KC = CD // 128
Q_PARTS = (0, 0, 0, 1, 1, 2)
K_PARTS = (0, 1, 2, 0, 1, 0)
KQ = 16 * len(Q_PARTS)
NATK = KQ
TRK = KQ + 4
LEAD = 11
SCALE = float(D) ** -0.5
EPS = 1e-12


class Plan:

    ENGINES = ("sync", "gpsimd", "scalar", "vector", "tensor")

    def __init__(self, per):
        self.ops = {e: [] for e in self.ENGINES}
        self.count, self.at, self.seen = {}, {}, {e: {} for e in self.ENGINES}
        self.period, self.per = -1, per
        self.starts = {}

    def start(self, period):
        self.period = period
        self.starts[period] = dict(self.count)

    def op(self, eng, fn, need=(), done=None, step=1):
        waits = []
        for label in need:
            if label is None:
                continue
            if label not in self.at:
                idx = label[1][0] if isinstance(label[1], tuple) else label[1]
                assert idx < 0, label
                continue
            kind, value = self.at[label]
            if self.seen[eng].get(kind, 0) < value:
                self.seen[eng][kind] = value
                waits.append((kind, value))
        if done is not None:
            kind, idx = done
            self.count[kind] = self.count.get(kind, 0) + step
            self.at[done] = (kind, self.count[kind])
            self.at[(kind.rstrip("01"), idx)] = (kind, self.count[kind])
            done = kind
        self.ops[eng].append((self.period, tuple(waits), fn, done, step))

    def same(self, p, q, grow):
        for e in self.ENGINES:
            a = [o for o in self.ops[e] if o[0] == p]
            b = [o for o in self.ops[e] if o[0] == q]
            if len(a) != len(b):
                return False
            for x, y in zip(a, b):
                if x[3] != y[3] or [w[0] for w in x[1]] != [w[0] for w in y[1]]:
                    return False
                if any(v + (q - p) * grow.get(k, 0) != w for (k, v), (_, w) in zip(x[1], y[1])):
                    return False
        return True

    def emit(self, nc, ctx):
        last = max(self.starts)
        first = None
        for f in range(1, last):
            grow = {k: self.starts[f + 1].get(k, 0) - self.starts[f].get(k, 0) for k in self.count}
            ends = [p for p in range(f + 1, last) if all(self.same(f, q, grow) for q in range(f + 1, p + 1))]
            if ends:
                first, end = f, ends[-1]
                break
        assert first is not None and end - first >= 4, (first, last)
        sems = {k: ctx.enter_context(nc.semaphore("s_" + k)) for k in self.count}
        gate = {k: ctx.enter_context(nc.semaphore("s_gate_" + k)) for k in ("sync", "gpsimd")}
        block = ctx.enter_context(nc.Block())

        def run(eng, period, i):
            for p, waits, fn, done, step in self.ops[eng[0]]:
                if p != period:
                    continue
                for k, v in waits:
                    eng[1].wait_ge(sems[k], v if i is None else v + i * grow[k])
                    if i is not None and eng[0] in ("sync", "gpsimd"):
                        eng[1].sem_inc(gate[eng[0]], 1)
                ins = fn(eng[1], (lambda b: b) if i is None else (lambda b: b + i * self.per))
                if done is not None:
                    ins.then_inc(sems[done], step)

        def program(name, e):
            for p in range(-1, first):
                run((name, e), p, None)
            if any(o[0] == first for o in self.ops[name]):
                with e.Fori(0, end - first + 1) as i:
                    run((name, e), first, i)
            for p in range(end + 1, last + 2):
                run((name, e), p, None)

        @block.sync
        def _(e):
            program("sync", e)
            for k, v in self.count.items():
                if k.startswith("store"):
                    e.wait_ge(sems[k], v)

        @block.gpsimd
        def _(e):
            program("gpsimd", e)

        @block.scalar
        def _(e):
            program("scalar", e)

        @block.vector
        def _(e):
            program("vector", e)

        @block.tensor
        def _(e):
            program("tensor", e)


def xattn_layer(nc, ctx, first_layer, x_nat, x_t, ctx_t, mask, wq, wk, wv, wki, wvi, wout, bias,
                ident_h, sel_h, kmask_h, vmask_h, parts_h, y_nat, y_t):
    NT = 77 if first_layer else T - 4
    NI = T - NT
    L0 = first_layer

    def sb(name, shape, dt=F32):
        return ctx.enter_context(nc.sbuf_tensor(name + ("_0" if L0 else "_1"), shape, dt))

    def bank(name):
        return ctx.enter_context(nc.psum_tensor(name + ("_0" if L0 else "_1"), [128, 512], F32))

    WQ = sb("WQ", [128, 3, C])
    WO = sb("WO", [128, 3, C])
    WK, WKI, WV, WVI = (sb(n, [128, KC, C]) for n in ("WK", "WKI", "WV", "WVI"))
    BIAS = sb("BIAS", [128, C])
    IDENT = sb("IDENT", [128, 128])
    MASK = sb("MASK", [128, 2])
    XT = sb("XT", [128, 2, 3, S])
    CT = sb("CT", [128, 2, KC, T])
    XN = sb("XN", [128, 2, 2, C])
    QKF = sb("QKF", [128, 3, 2 * S])
    RES = sb("RES", [128, 2 * S])
    PARTS = sb("PARTS", [128, 3, 3, 2 * S], BF16)
    QS = sb("QS", [TRK, 2, H, S], BF16)
    KS = sb("KS", [TRK, 2, H, T], BF16)
    MX = sb("MX", [128, 2, 2, 8])
    NH = sb("NH", [8, 2, 2, S], BF16)
    NP = 8
    P = sb("P", [128, NP, 2 * S])
    PVS = sb("PVS", [128, 2 * S])
    ON = sb("ON", [128, 2, 2, 2, H * SLOT])
    HS = sb("HS", [128, 2, C])
    HT = sb("HT", [128, 3, S])
    Y = sb("Y", [128, 2, C])
    XB = sb("XB", [128, 2, C])
    R1 = sb("R1", [128, 2, 2, H])
    VB = sb("VB", [128, 2, 2, H, SLOT])
    if L0:
        VA = sb("VA", [NT, 2, H, SLOT])
        CZ = sb("CZ", [128, KC, 128])
        IPONE = sb("IPONE", [128, H])
        G0 = sb("G0", [NT, T])
        TPM = sb("TPM", [128, 4, 2])
        TP = sb("TP", [128, 2, NT])
        TPN = sb("TPN", [128, 2, NT])
        TPT = sb("TPT", [NT, S])
        SN = sb("SN", [128, 2, 2, NI])
        ST = sb("ST", [128, 2, 2 * S])
        TMP = sb("TMP", [128, 2, 2, NI])
        TA = sb("TA", [128, 2, 2 * S])
        YT = sb("YT", [128, 3, S])
    else:
        GL = sb("GL", [128, 2, 3, 128])
        E21 = sb("E21", [128, SLOT])
        ONES = sb("ONES", [128, 128])
        ZP = sb("ZP", [128, NP, 2 * S])
        SQ = sb("SQ", [128, KC, 4])
        CIP = sb("CIP", [128, KC, 80])
        RN = sb("RN", [128, 3, 4])
        RNI = sb("RNI", [128, 2, 4])
        KMASK = sb("KMASK", [128, 8, 4])
        KBD = sb("KBD", [128, 3, 8, 4])
        VMASK = sb("VMASK", [80, C])
        VIP = sb("VIP", [80, 2, C])
        SC = sb("SC", [128, 2, 2, 80])
        HALF = sb("HALF", [128, 2, H])
        NRM = sb("NRM", [128, 4, 2, H])
        FU = sb("FU", [128, 6, 2, 80])
        FM = sb("FM", [128, 4, 2, H])
        PT = sb("PT", [80, S])

    NAT = [bank(f"NAT{k}") for k in range(2)]
    TR = [bank(f"TR{k}") for k in range(2)]
    PV = bank("PV")
    n_misc = 3 if L0 else 2
    MISC = [bank(f"MISC{k}") for k in range(n_misc)]
    if not L0:
        GP = bank("GP")

    pl = Plan(2)
    op = pl.op
    qk_bank = {}
    misc_state = {"n": 0, "last": [None] * n_misc}

    def misc():
        k = misc_state["n"] % n_misc
        misc_state["n"] += 1
        return k, misc_state["last"][k]

    def free_after(k, label):
        misc_state["last"][k] = label

    def setup():
        n_w = 0
        def load(dst, src):
            op("sync", lambda e, bx: e.dma_start(dst, src), done=("w", 0), step=16)
        for c, (c0, cn) in enumerate(CC):
            load(WQ[0:cn, c, :], wq[c0:c0 + cn, :])
            load(WO[0:cn, c, :], wout[c0:c0 + cn, :])
        for w_sb, w_dr in ((WK, wk), (WKI, wki), (WV, wv), (WVI, wvi)):
            load(w_sb[:, :, :], w_dr.rearrange("(k p) n -> p k n", p=128))
        load(BIAS[:, :], bias)
        load(IDENT[:, :], ident_h)
        load(MASK[:, :], mask)
        for par in range(2):
            load(KS[KQ:TRK, par, :, :], sel_h)
        if not L0:
            load(KMASK[:, :, :], kmask_h)
            load(VMASK[:, :], vmask_h)
        ms = lambda ap, v: op("vector", lambda e, bx: e.memset(ap, v), done=("init", 0))
        ms(QS[KQ:TRK, :, :, :], 0.0)
        ms(VB[:, :, :, :, :], 0.0)
        if L0:
            ms(VA[:, :, :, :], 0.0)
            op("vector", lambda e, bx: e.memset(VA[:, :, :, D:D + 1], 1.0), need=[("init", 0)], done=("init", 0))
            ms(G0[:, :], 0.0)
            ms(CZ[:, :, :], 0.0)
            load(IPONE[:, :], vmask_h)
            op("vector", lambda e, bx: e.tensor_copy(VB[:, :, 0, :, D], IPONE[:, :].unsqueeze(1).broadcast_to([128, 2, H])),
               need=[("w", 0), ("init", 0)], done=("init", 0))
            op("vector", lambda e, bx: e.memset(VB[:, :, 1, :, D:D + 1], 1.0), need=[("init", 0)], done=("init", 0))
        else:
            ms(KS[0:KQ, :, :, NT:T], 0.0)
            ms(GL[:, :, :, :], 0.0)
            ms(E21[:, :], 0.0)
            ms(ONES[:, :], 1.0)
            ms(HALF[:, :, :], 0.5)
            ms(KBD[:, :, :, :], 0.0)
            op("vector", lambda e, bx: e.memset(E21[:, 21:22], 1.0), need=[("init", 0)], done=("init", 0))
            op("vector", lambda e, bx: e.memset(VB[:, :, 0, :, D:D + 1], 1.0), done=("init", 0))
            op("vector", lambda e, bx: e.memset(VB[0:NT - 128, :, 1, :, D:D + 1], 1.0), done=("init", 0))
        op("tensor", lambda e, bx: e.transpose(MISC[0][:, 0:128], IDENT[:, :], IDENT[:, :]),
           need=[("w", 0), ("init", 0)], done=("warm", 0))

    READY = [("w", 0), ("init", 0)]

    def loads(b):
        p = b % 2
        for c, (c0, cn) in enumerate(CC):
            op("sync", lambda e, bx, c=c, c0=c0, cn=cn: e.dma_start(XT[0:cn, p, c, :], x_t[bx(b), c0:c0 + cn, :]),
               need=[("qk", (b - 2, 2))], done=(f"ld{p}", b), step=16)
        op("sync", lambda e, bx: e.dma_start(CT[:, p, :, :], ctx_t[bx(b)].rearrange("(k q) t -> q k t", q=128)),
           need=[("ctlast", b - 2), ("ctpool", b - 2)], done=(f"ld{p}", b), step=16)

    def load_residual(b):
        p = b % 2
        op("sync", lambda e, bx: e.dma_start(XN[:, p, :, :], x_nat[bx(b)].rearrange("(a q) c -> q a c", q=128)),
           need=[("xb", b - 2)], done=(f"xn{p}", b), step=16)

    def group(out, pairs, need, done=None):
        for n, (lhs, rhs) in enumerate(pairs):
            op("tensor", lambda e, bx, n=n, lhs=lhs, rhs=rhs: e.matmul(
                out, lhs, rhs, start=(n == 0), stop=(n == len(pairs) - 1)),
               need=need if n == 0 else (), done=done if n == len(pairs) - 1 else None)

    def project_q(b, m):
        p, (m0, mn) = b % 2, MT[m]
        qk_bank[m], last = misc()
        group(MISC[qk_bank[m]][0:mn, 0:S], [(WQ[0:cn, c, m0:m0 + mn], XT[0:cn, p, c, :]) for c, (_, cn) in enumerate(CC)],
              READY + [("ld", b), last])
        free_after(qk_bank[m], ("qkh", (b, m)))

    def project_k(b, m):
        p, (m0, mn), k = b % 2, MT[m], qk_bank[m]
        group(MISC[k][0:mn, S:S + NT], [(WK[:, c, m0:m0 + mn], CT[:, p, c, 0:NT]) for c in range(KC)], ())
        group(MISC[k][0:mn, S + NT:S + T], [(WKI[:, c, m0:m0 + mn], CT[:, p, c, NT:T]) for c in range(KC)], (),
              ("qk", (b, m)))
        op("scalar", lambda e, bx: e.copy(QKF[0:mn, m, :], MISC[k][0:mn, :]),
           need=[("qk", (b, m)), ("parts", (b - 1, m)), ("qkfread", b - 1)], done=("qkf", (b, m)))
        op("scalar", lambda e, bx: e.copy(PARTS[0:mn, m, 0, :], MISC[k][0:mn, :]),
           need=[("spill", b - 1)], done=("qkh", (b, m)))
        op("gpsimd", lambda e, bx: e.tensor_tensor(RES[0:mn, :], QKF[0:mn, m, :], PARTS[0:mn, m, 0, :], ALU.subtract),
           need=[("qkh", (b, m)), ("parts", (b, m - 1) if m else (b - 1, 2))], done=("split", (b, m)))

    def split_rest(b, m):
        mn = MT[m][1]
        op("scalar", lambda e, bx: e.copy(PARTS[0:mn, m, 1, :], RES[0:mn, :]), need=[("split", (b, m))], done=("split2", (b, m)))
        op("gpsimd", lambda e, bx: e.tensor_tensor(PARTS[0:mn, m, 2, :], RES[0:mn, :], PARTS[0:mn, m, 1, :], ALU.subtract),
           need=[("split2", (b, m))], done=("parts", (b, m)))

    def spill_parts(b):
        p = b % 2
        for m, (m0, mn) in enumerate(MT):
            for qk in range(2):
                op("sync", lambda e, bx, m=m, m0=m0, mn=mn, qk=qk: e.dma_start(
                    parts_h[p, qk, :, m0:m0 + mn, :].rearrange("j r t -> r j t"),
                    PARTS[0:mn, m, :, qk * S:(qk + 1) * S]),
                   need=[("parts", (b, m)), ("stack", b - 2)], done=("spill", b), step=16)

    def stack_parts(b):
        p = b % 2
        for r in range(len(Q_PARTS)):
            for qk, dst, parts, n in ((0, QS, Q_PARTS, S), (1, KS, K_PARTS, T if L0 else NT)):
                op("sync", lambda e, bx, r=r, qk=qk, dst=dst, parts=parts, n=n: e.dma_start(
                    dst[16 * r:16 * r + 16, p, :, 0:n],
                    parts_h[p, qk, parts[r], :, 0:n].rearrange("(h d) t -> d h t", d=D)),
                   need=[("spill", b), ("trans", 20 * (b - 2) + 19)] + READY, done=(f"stack{p}", b), step=16)

    def project_v(b, which):
        p = b % 2
        k, last = misc()
        tag = ("vmm", (b, which))
        need = READY + [("ld", b), last] + ([("cz", b)] if L0 else [])
        if L0:
            lhs, w, n, dst = {
                0: (lambda c: CT[:, p, c, 0:NT], WV, NT, VA[:, p, :, 0:D]),
                1: (lambda c: CZ[:, c, :], WVI, 128, VB[:, p, 0, :, 0:D]),
                2: (lambda c: CT[:, p, c, 128:T], WVI, 128, VB[:, p, 1, :, 0:D]),
            }[which]
        else:
            lhs, w, n, dst = {
                0: (lambda c: CT[:, p, c, 0:128], WV, 128, VB[:, p, 0, :, 0:D]),
                1: (lambda c: CT[:, p, c, 128:NT], WV, NT - 128, VB[0:NT - 128, p, 1, :, 0:D]),
            }[which]
        group(MISC[k][0:n, 0:C], [(lhs(c), w[:, c, :]) for c in range(KC)], need, tag)
        src = MISC[k][0:n, 0:C].rearrange("p (h d) -> p h d", d=D)
        op("scalar", lambda e, bx: e.copy(dst, src), need=[tag, ("pv", (b - 2, 4))] + READY, done=("v", b))
        pl.at[("vs", (b, which))] = pl.at[("v", b)]
        free_after(k, ("vs", (b, which)))
        if which == (2 if L0 else 1):
            pl.at[("ctlast", b)] = pl.at[tag]

    def clear_text(b):
        op("gpsimd", lambda e, bx: e.tensor_copy(CZ[:, :, NT:128], CT[:, b % 2, :, NT:128]),
           need=READY + [("ld", b), ("ctlast", b - 1)], done=("cz", b))
        pl.at[("ctpool", b)] = pl.at[("cz", b)]

    def text_logits(b):
        k, last = misc()
        for a in range(2):
            group(MISC[k][:, a * NT:(a + 1) * NT],
                  [(QKF[0:mn, m, a * 128:(a + 1) * 128], QKF[0:mn, m, S:S + NT]) for m, (_, mn) in enumerate(MT)],
                  [("qkf", (b, 2)), last], ("tl", b))
        pl.at[("qkfread", b)] = pl.at[("tl", b)]
        lg = MISC[k][:, 0:2 * NT].rearrange("p (a t) -> p a t", a=2)
        op("vector", lambda e, bx: e.tensor_reduce(TPM[:, 0, :], lg, AX.X, ALU.max, negate=True),
           need=[("tl", b), ("tpn", b - 1)], done=("tmax", b))
        op("vector", lambda e, bx: e.tensor_scalar(TPM[:, 1, :], TPM[:, 0, :], SCALE, None, ALU.mult),
           need=[("tmax", b), ("texp", b - 1)], done=("tbias", b))
        for a in range(2):
            op("scalar", lambda e, bx, a=a: e.activation(TP[:, a, :], MISC[k][:, a * NT:(a + 1) * NT], ACT.Exp,
                                                         bias=TPM[:, 1, a:a + 1], scale=SCALE,
                                                         accum_out=TPM[:, 2, a:a + 1]),
               need=[("tbias", b), ("tpn", b - 1)], done=("texp", b))
        free_after(k, ("texp", b))
        op("vector", lambda e, bx: e.reciprocal(TPM[:, 3, :], TPM[:, 2, :]), need=[("texp", b), ("tpn", b - 1)], done=("trz", b))
        op("vector", lambda e, bx: e.tensor_tensor(TPN[:, :, :], TP[:, :, :],
                                                   TPM[:, 3, :].unsqueeze(2).broadcast_to([128, 2, NT]), ALU.mult),
           need=[("trz", b), ("tpt", b - 1)], done=("tpn", b))

    def gram_text_ip(b):
        k, last = misc()
        group(MISC[k][0:NT, 0:NI], [(CT[:, b % 2, c, 0:NT], CT[:, b % 2, c, NT:T]) for c in range(KC)],
              READY + [("ld", b), last], ("g0", b))
        op("scalar", lambda e, bx: e.mul(G0[:, NT:T], MISC[k][0:NT, 0:NI], 0.5),
           need=[("g0", b), ("stmm", b - 1)] + READY, done=("g0s", b))
        free_after(k, ("g0s", b))

    def probs_t(b):
        k, last = misc()
        for a in range(2):
            op("tensor", lambda e, bx, a=a: e.transpose(MISC[k][0:NT, a * 128:(a + 1) * 128], TPN[:, a, :], IDENT[:, :]),
               need=[("tpn", b), last], done=("tpt", b))
        op("scalar", lambda e, bx: e.copy(TPT[:, :], MISC[k][0:NT, 0:S]), need=[("tpt", b), ("stmm", b - 1)], done=("tpts", b))
        free_after(k, ("tpts", b))

    def sem_natural(b):
        k, last = misc()
        for a in range(2):
            group(MISC[k][:, a * NI:(a + 1) * NI], [(TPT[:, a * 128:(a + 1) * 128], G0[:, NT:T])],
                  [("tpts", b), ("g0s", b), last], ("snmm", b))
        op("scalar", lambda e, bx: e.copy(SN[:, b % 2, :, :], MISC[k][:, 0:2 * NI].rearrange("p (a t) -> p a t", a=2)),
           need=[("snmm", b), ("max", 20 * (b - 2) + 19)], done=("sn", b))
        free_after(k, ("sn", b))

    def sem_transposed(b):
        k, last = misc()
        for a in range(2):
            group(MISC[k][:, a * S:(a + 1) * S], [(G0[:, a * 128:(a + 1) * 128], TPT[:, :])], [last], ("stmm", b))
        op("scalar", lambda e, bx: e.copy(ST[:, b % 2, :], MISC[k][:, :]),
           need=[("stmm", b), ("sadd", 20 * (b - 2) + 19)], done=("st", b))
        free_after(k, ("st", b))

    def gram(b, which):
        p = b % 2
        k, last = misc()
        need = READY + [("ld", b), last]
        if which == 0:
            group(MISC[k][:, 0:128], [(CT[:, p, c, 0:128], CT[:, p, c, 0:128]) for c in range(KC)], need)
            group(MISC[k][:, 128:132], [(CT[:, p, c, 0:128], CT[:, p, c, NT:T]) for c in range(KC)], (), ("gr", (b, 0)))
            jobs = [(GL[:, p, 0, :], MISC[k][:, 0:128], 1.0)]
            n, c0, tt = 128, 128, 0
        else:
            n, c0, tt = NT - 128, NT, 1
            group(MISC[k][0:n, 0:T], [(CT[:, p, c, 128:NT], CT[:, p, c, :]) for c in range(KC)], need, ("gr", (b, 1)))
            jobs = [(GL[0:n, p, 1, :], MISC[k][0:n, 0:128], 2.0), (GL[0:n, p, 2, 0:n], MISC[k][0:n, 128:NT], 1.0)]
        for dst, src, f in jobs:
            op("scalar", lambda e, bx, dst=dst, src=src, f=f: e.mul(dst, src, f),
               need=[("gr", (b, which)), ("gpmm", 20 * (b - 2) + 19)] + READY, done=("gl", b))
        op("scalar", lambda e, bx: e.copy(VB[0:n, p, tt, :, D + 1:D + 5],
                                          MISC[k][0:n, c0:c0 + 4].unsqueeze(1).broadcast_to([n, H, 4])),
           need=[("pv", (b - 2, 4))], done=("gl", b))
        pl.at[("gl", (b, which))] = pl.at[("gl", b)]
        free_after(k, ("gl", (b, which)))

    def ip_copies(b):
        p = b % 2
        ipc = CT[:, p, :, NT:T]
        op("gpsimd", lambda e, bx: e.tensor_tensor(SQ[:, :, :], ipc, ipc, ALU.mult),
           need=READY + [("ld", b), ("rnmm", b - 1)], done=("cip", b))
        op("gpsimd", lambda e, bx: e.tensor_copy(CIP[:, :, :].rearrange("p k (h n) -> p k h n", n=4),
                                                 ipc.unsqueeze(2).broadcast_to([128, KC, H, 4])),
           need=[("vipmm", b - 1)], done=("cip", b))
        pl.at[("ctpool", b)] = pl.at[("cip", b)]

    def ip_values(b):
        k, last = misc()
        group(MISC[k][0:80, 0:C], [(CIP[:, c, :], WVI[:, c, :]) for c in range(KC)], [("cip", b), last], ("vipmm", b))
        op("vector", lambda e, bx: e.tensor_tensor(VIP[:, b % 2, :], MISC[k][0:80, 0:C], VMASK[:, :], ALU.mult),
           need=READY + [("vipmm", b), ("ipmm", (b - 2, 1))], done=("vip", b))
        free_after(k, ("vip", b))

    def ip_norms(b):
        k, last = misc()
        group(MISC[k][:, 0:4], [(ONES[:, :], SQ[:, c, :]) for c in range(KC)], [("cip", b), last], ("rnmm", b))
        op("vector", lambda e, bx: e.tensor_copy(RN[:, 0, :], MISC[k][:, 0:4]), need=[("rnmm", b), ("rn", (b - 1, 1))], done=("rn", (b, 0)))
        free_after(k, ("rn", (b, 0)))
        op("gpsimd", lambda e, bx: e.tensor_tensor(RN[:, 1, :], RN[:, 0, :], HALF[:, 0, 0:4], ALU.pow),
           need=READY + [("rn", (b, 0)), ("rn", (b - 1, 2))], done=("rn1", b))
        op("vector", lambda e, bx: e.tensor_scalar(RN[:, 2, :], RN[:, 1, :], EPS, None, ALU.max),
           need=[("rn1", b), ("rn", (b - 1, 2))], done=("rn", (b, 1)))
        op("vector", lambda e, bx: e.reciprocal(RNI[:, b % 2, :], RN[:, 2, :]), need=[("rn", (b, 1)), ("fu", (b - 2, 0))], done=("rn", (b, 2)))

    def ip_scores(b):
        op("vector", lambda e, bx: e.tensor_tensor(
            KBD[:, 0:2, :, :], KMASK[:, :, :].unsqueeze(1).broadcast_to([128, 2, 8, 4]),
            QKF[:, 0:2, S + NT:S + T].unsqueeze(2).broadcast_to([128, 2, 8, 4]), ALU.mult),
           need=READY + [("qkf", (b, 2)), ("scmm", b - 1)], done=("kbd", b))
        op("vector", lambda e, bx: e.tensor_tensor(
            KBD[0:64, 2, :, :], KMASK[0:64, :, :], QKF[0:64, 2, S + NT:S + T].unsqueeze(1).broadcast_to([64, 8, 4]),
            ALU.mult), done=("kbd", b))
        k, last = misc()
        for a in range(2):
            for m, (_, mn) in enumerate(MT):
                w = mn // 4
                group(MISC[k][:, a * 80 + m * 32:a * 80 + m * 32 + w],
                      [(QKF[0:mn, m, a * 128:(a + 1) * 128], KBD[0:mn, m, 0:w // 4, :])],
                      [("kbd", b), last], ("scmm", b))
        pl.at[("qkfread", b)] = pl.at[("scmm", b)]
        op("vector", lambda e, bx: e.tensor_scalar(SC[:, b % 2, :, :], MISC[k][:, 0:160].rearrange("p (a n) -> p a n", a=2),
                                                   SCALE, None, ALU.mult),
           need=[("scmm", b), ("fu", (b - 2, 1))], done=("sc", b))
        free_after(k, ("sc", b))

    def maxima(s):
        b, h = divmod(s, H)
        p, k, gp, j = b % 2, s % 2, (s // HG) % 2, h % HG
        for a in range(2):
            op("tensor", lambda e, bx, a=a: e.matmul(
                NAT[k][:, a * T:(a + 1) * T], QS[0:NATK, p, h, a * 128:(a + 1) * 128], KS[0:NATK, p, h, :],
                start=True, stop=True),
               need=READY + [("stack", b), ("max", s - 2)], done=("nat", s))
        v = NAT[k][:, :].rearrange("p (a t) -> p a t", a=2)
        if L0:
            op("vector", lambda e, bx: e.tensor_tensor(TMP[:, k, :, :], v[:, :, NT:T], SN[:, p, :, :], ALU.add),
               need=[("nat", s), ("sn", b), ("max", s - 2)], done=("nadd", s))
        op("vector", lambda e, bx: e.tensor_reduce(MX[:, gp, :, j], v[:, :, 0:NT], AX.X, ALU.max, negate=True),
           need=[("nat", s), ("mxt", s // HG - 2)], done=None if L0 else ("max", s))
        if L0:
            op("vector", lambda e, bx: e.tensor_reduce(MX[:, gp, :, HG + j], TMP[:, k, :, :], AX.X, ALU.max, negate=True),
               need=[("nadd", s)], done=("max", s))

    def max_rows(g):
        b, hg = divmod(g, H // HG)
        gp, p = g % 2, b % 2
        w = 8 if L0 else 4
        k, last = misc()
        for a in range(2):
            op("tensor", lambda e, bx, a=a: e.transpose(MISC[k][0:w, a * 128:(a + 1) * 128], MX[:, gp, a, 0:w], IDENT[:, :]),
               need=[("max", HG * g + HG - 1), last], done=("mxt", g))
        op("vector", lambda e, bx: e.tensor_copy(NH[0:w, gp, 0, :], MISC[k][0:w, 0:S]),
           need=[("mxt", g), ("mrow", g - 2)], done=("nh", g))
        op("vector", lambda e, bx: e.tensor_tensor(NH[0:w, gp, 1, :], MISC[k][0:w, 0:S], NH[0:w, gp, 0, :], ALU.subtract),
           need=[("nh", g)], done=("nm", g))
        free_after(k, ("nm", g))
        for part in range(2):
            for grp in range(w // HG):
                r = KQ + 2 * part + grp
                op("sync", lambda e, bx, part=part, grp=grp, r=r: e.dma_start(
                    QS[r:r + 1, p, HG * hg:HG * hg + HG, :], NH[HG * grp:HG * grp + HG, gp, part, :]),
                   need=READY + [("nm", g), ("trans", HG * (g - 10) + 3)], done=(f"mrow{gp}", g), step=16)

    def exponentials(s):
        b, h = divmod(s, H)
        p, k = b % 2, s % 2
        for a in range(2):
            op("tensor", lambda e, bx, a=a: e.matmul(
                TR[k][:, a * S:(a + 1) * S], KS[0:TRK, p, h, a * 128:(a + 1) * 128], QS[0:TRK, p, h, :],
                start=True, stop=True),
               need=READY + [("stack", b), ("mrow", s // HG), ("sadd" if L0 else "exp", s - 2)], done=("trans", s))
        if L0:
            op("vector", lambda e, bx: e.tensor_tensor(TA[:, k, :], TR[k][:, :], ST[:, p, :], ALU.add),
               need=[("trans", s), ("st", b), ("exp", s - 2)], done=("sadd", s))
        op("scalar", lambda e, bx: e.activation(P[:, s % NP, :], TA[:, k, :] if L0 else TR[k][:, :], ACT.Exp, scale=SCALE),
           need=[("sadd" if L0 else "trans", s), ("pv", divmod((s - NP) // HG, H // HG))],
           done=("exp", s))

    def quadratic(s):
        b, h = divmod(s, H)
        p, r = b % 2, s % NP
        n2 = NT - 128
        p0, p1 = P[:, r, 0:S], P[0:n2, r, S:2 * S]
        group(GP[:, 0:S], [(GL[:, p, 0, :], p0), (GL[0:n2, p, 1, :], p1)], [("exp", s), ("gl", b), ("zp", s - 1)])
        group(GP[:, S:2 * S], [(GL[0:n2, p, 2, :], p1)], (), ("gpmm", s))
        op("vector", lambda e, bx: e.tensor_tensor(ZP[:, r, :], GP[:, :], P[:, r, :], ALU.mult),
           need=[("gpmm", s), ("pv", divmod((s - NP) // HG, H // HG))], done=("zp", s))

    def weighted_sums(g):
        b, hg = divmod(g, H // HG)
        p = b % 2
        lab = ("pv", (b, hg))
        need = [("exp", HG * g + HG - 1), ("v", b), ("pvs", g - 1)]
        rounds = []
        if L0:
            rounds.append([(PV[SLOT * j:SLOT * (j + 1), 0:S], VA[:, p, HG * hg + j, :], P[0:NT, (HG * g + j) % NP, 0:S], True, True)
                           for j in range(HG)])
            for tt in range(2):
                rounds.append([(PV[SLOT * j:SLOT * (j + 1), S:2 * S], VB[:, p, tt, HG * hg + j, :],
                                P[:, (HG * g + j) % NP, tt * S:(tt + 1) * S], tt == 0, tt == 1) for j in range(HG)])
        else:
            need.append(("gl", b))
            need.append(("zp", HG * g + HG - 1))
            for tt in range(2):
                rounds.append([(PV[SLOT * j:SLOT * (j + 1), 0:S], VB[:, p, tt, HG * hg + j, :],
                                P[:, (HG * g + j) % NP, tt * S:(tt + 1) * S], tt == 0, False) for j in range(HG)])
            for tt in range(2):
                rounds.append([(PV[SLOT * j:SLOT * (j + 1), 0:S], E21[:, :],
                                ZP[:, (HG * g + j) % NP, tt * S:(tt + 1) * S], False, tt == 1) for j in range(HG)])
        flat = [x for r in rounds for x in r]
        for n, (out, lhs, rhs, st, sp) in enumerate(flat):
            op("tensor", lambda e, bx, out=out, lhs=lhs, rhs=rhs, st=st, sp=sp: e.matmul(out, lhs, rhs, start=st, stop=sp),
               need=need if n == 0 else (), done=lab if n == len(flat) - 1 else None)
        w = 2 * S if L0 else S
        op("scalar", lambda e, bx: e.copy(PVS[:, 0:w], PV[:, 0:w]), need=[lab, ("ont", g - 1)], done=("pvs", g))

    def to_natural(g):
        b, hg = divmod(g, H // HG)
        k, last = misc()
        n = 4 if L0 else 2
        for a in range(n):
            op("tensor", lambda e, bx, a=a: e.transpose(MISC[k][:, a * 128:(a + 1) * 128], PVS[:, a * 128:(a + 1) * 128], IDENT[:, :]),
               need=[("pvs", g), last], done=("ont", g))
        op("scalar", lambda e, bx: e.copy(
            ON[:, b % 2, 0:n // 2, :, 128 * hg:128 * (hg + 1)],
            MISC[k][:, 0:n * 128].rearrange("p (v a n) -> p v a n", v=n // 2, a=2)),
           need=[("ont", g), ("hs", b - 2)], done=("on", g))
        free_after(k, ("on", g))

    def on_view(b, v):
        return ON[:, b % 2, v, :, :].rearrange("p a (h s) -> p a h s", s=SLOT)

    def residual(b):
        op("gpsimd", lambda e, bx: e.tensor_tensor(XB[:, :, :], XN[:, b % 2, :, :],
                                                   BIAS[:, :].unsqueeze(1).broadcast_to([128, 2, C]), ALU.add),
           need=READY + [("xn", b), ("y", (b - 1, 1))], done=("xb", b))

    HSV = HS[:, :, :].rearrange("p a (h d) -> p a h d", d=D)

    def combine_l0(b):
        A_, B_ = on_view(b, 0), on_view(b, 1)
        g = 5 * b + 4
        op("vector", lambda e, bx: e.reciprocal(R1[:, 0, :, :], A_[:, :, :, D]), need=[("on", g), ("hs", b - 1)], done=("cmb", (b, 0)))
        op("vector", lambda e, bx: e.reciprocal(R1[:, 1, :, :], B_[:, :, :, D]), done=("cmb", (b, 1)))
        for a in range(2):
            op("vector", lambda e, bx, a=a: e.tensor_scalar(R1[:, 1, a, :], R1[:, 1, a, :], MASK[:, a:a + 1], None, ALU.mult),
               need=READY + [("cmb", (b, 1))], done=("cmb", (b, 2)))
        bc = lambda v: R1[:, v, :, :].unsqueeze(3).broadcast_to([128, 2, H, D])
        for v, X in enumerate((A_, B_)):
            op("vector", lambda e, bx, v=v, X=X: e.tensor_tensor(X[:, :, :, 0:D], X[:, :, :, 0:D], bc(v), ALU.mult),
               need=[("cmb", (b, 2))], done=("cmb", (b, 3)))
        op("vector", lambda e, bx: e.tensor_tensor(HSV, A_[:, :, :, 0:D], B_[:, :, :, 0:D], ALU.add),
           need=[("cmb", (b, 3)), ("hst", (b - 1, 1))], done=("hs", b))

    def combine_l1(b, stage):
        A_ = on_view(b, 0)
        g = 5 * b + 4
        V = lambda fn, need=(), done=None: op("vector", fn, need=need, done=done) if stage == now[0] else None
        q = b % 2
        now = [0]
        rz = R1[:, 0, :, :]
        V(lambda e, bx: e.reciprocal(rz, A_[:, :, :, D]), [("on", g), ("hs", b - 1), ("fu", (b - 1, 0))], ("cmb", (b, 0)))
        V(lambda e, bx: e.tensor_scalar(NRM[:, 0, :, :], A_[:, :, :, D + 5], 0.0, None, ALU.max), [("nrm", b - 1)], ("cmb", (b, 1)))
        if stage == 0:
          op("gpsimd", lambda e, bx: e.tensor_tensor(NRM[:, 1, :, :], NRM[:, 0, :, :], HALF[:, :, :], ALU.pow),
           need=READY + [("cmb", (b, 1)), ("cmb", (b - 1, 2))], done=("nrm", b))
        now[0] = 1
        V(lambda e, bx: e.tensor_tensor(NRM[:, 2, :, :], NRM[:, 1, :, :], rz, ALU.mult), [("nrm", b), ("cmb", (b - 1, 3))], ("cmb", (b, 2)))
        V(lambda e, bx: e.tensor_scalar(NRM[:, 2, :, :], NRM[:, 2, :, :], EPS, None, ALU.max), [("cmb", (b, 2))], ("cmb", (b, 3)))
        V(lambda e, bx: e.reciprocal(NRM[:, 3, :, :], NRM[:, 2, :, :]), [("cmb", (b, 3)), ("cmb", (b - 1, 5))], ("cmb", (b, 4)))
        V(lambda e, bx: e.scalar_tensor_tensor(NRM[:, 3, :, :], NRM[:, 3, :, :], 0.5, rz, ALU.mult, ALU.mult), [("cmb", (b, 4))], ("cmb", (b, 5)))
        F = lambda i: FU[:, i, :, :].rearrange("p a (h n) -> p a h n", n=4)
        V(lambda e, bx: e.tensor_tensor(F(0), A_[:, :, :, D + 1:D + 5], NRM[:, 3, :, :].unsqueeze(3).broadcast_to([128, 2, H, 4]), ALU.mult),
          [("cmb", (b, 5)), ("fu", (b - 1, 0))], ("f1", b))
        V(lambda e, bx: e.tensor_tensor(FU[:, 1, :, :].rearrange("p a (h n) -> p (a h) n", n=4),
                                        FU[:, 0, :, :].rearrange("p a (h n) -> p (a h) n", n=4),
                                        RNI[:, q, :].unsqueeze(1).broadcast_to([128, 2 * H, 4]), ALU.mult),
          [("f1", b), ("rn", (b, 2)), ("fu", (b - 1, 1))], ("fu", (b, 0)))
        V(lambda e, bx: e.tensor_tensor(FU[:, 2, :, :], FU[:, 1, :, :], SC[:, q, :, :], ALU.add), [("fu", (b, 0)), ("sc", b), ("fu", (b - 1, 2))], ("fu", (b, 1)))
        V(lambda e, bx: e.tensor_reduce(FM[:, 0, :, :], F(2), AX.X, ALU.max), [("fu", (b, 1)), ("fu", (b - 1, 2))], ("f2", b))
        V(lambda e, bx: e.tensor_tensor(F(3), F(2), FM[:, 0, :, :].unsqueeze(3).broadcast_to([128, 2, H, 4]), ALU.subtract),
          [("f2", b), ("fexp", b - 1)], ("fu", (b, 2)))
        if stage == 1:
          op("scalar", lambda e, bx: e.activation(FU[:, 4, :, :], FU[:, 3, :, :], ACT.Exp), need=[("fu", (b, 2)), ("fu", (b - 1, 4))], done=("fexp", b))
        now[0] = 2
        V(lambda e, bx: e.tensor_reduce(FM[:, 1, :, :], F(4), AX.X, ALU.add), [("fexp", b), ("fu", (b - 1, 3))], ("f3", b))
        V(lambda e, bx: e.reciprocal(FM[:, 2, :, :], FM[:, 1, :, :]), [("f3", b), ("fu", (b - 1, 3))], ("f4", b))
        for a in range(2):
            V(lambda e, bx, a=a: e.tensor_scalar(FM[:, 3, a, :], FM[:, 2, a, :], MASK[:, a:a + 1], None, ALU.mult),
              READY + [("f4", b), ("fu", (b - 1, 4))], ("fu", (b, 3)))
        V(lambda e, bx: e.tensor_tensor(F(5), F(4), FM[:, 3, :, :].unsqueeze(3).broadcast_to([128, 2, H, 4]), ALU.mult),
          [("fu", (b, 3)), ("ptt", b - 1)], ("fu", (b, 4)))
        V(lambda e, bx: e.tensor_tensor(HSV, A_[:, :, :, 0:D], rz.unsqueeze(3).broadcast_to([128, 2, H, D]), ALU.mult),
          [("hst", (b - 1, 1))], ("tx", b))

    def ip_probs_t(b):
        k, last = misc()
        for a in range(2):
            op("tensor", lambda e, bx, a=a: e.transpose(MISC[k][0:80, a * 128:(a + 1) * 128], FU[:, 5, a, :], IDENT[:, :]),
               need=[("fu", (b, 4)), last], done=("ptt", b))
        op("scalar", lambda e, bx: e.copy(PT[:, :], MISC[k][0:80, 0:S]), need=[("ptt", b), ("ipmm", (b - 1, 1))], done=("pt", b))
        free_after(k, ("pt", b))

    def ip_out(b, a):
        k, last = misc()
        group(MISC[k][:, 0:C], [(PT[:, a * 128:(a + 1) * 128], VIP[:, b % 2, :])], [("pt", b), ("vip", b), last], ("ipmm", (b, a)))
        op("vector", lambda e, bx: e.tensor_tensor(HS[:, a, :], HS[:, a, :], MISC[k][:, 0:C], ALU.add),
           need=[("ipmm", (b, a)), ("tx", b)], done=("hs", b))
        pl.at[("hsa", (b, a))] = pl.at[("hs", b)]
        free_after(k, ("hsa", (b, a)))

    def hs_t(b, a):
        k, last = misc()
        for c, (c0, cn) in enumerate(CC):
            op("tensor", lambda e, bx, c=c, c0=c0, cn=cn: e.transpose(MISC[k][0:cn, c * 128:(c + 1) * 128], HS[:, a, c0:c0 + cn], IDENT[:, :]),
               need=[("hs", b), last], done=("hst", (b, a)))
        src = MISC[k][0:106, 0:384].rearrange("p (c q) -> p c q", c=3)
        op("scalar", lambda e, bx: e.copy(HT[0:106, :, a * 128:(a + 1) * 128], src),
           need=[("hst", (b, a)), ("omm", (b - 1, 1))], done=("ht", (b, a)))
        op("scalar", lambda e, bx: e.copy(HT[96:107, 0:2, a * 128:(a + 1) * 128],
                                          MISC[k][96:107, 0:256].rearrange("p (c q) -> p c q", c=2)),
           need=[("ht", (b, a))], done=("ht2", (b, a)))
        free_after(k, ("ht2", (b, a)))

    def project_out(b, a):
        k, last = misc()
        group(MISC[k][:, 0:C], [(HT[0:cn, c, a * 128:(a + 1) * 128], WO[0:cn, c, :]) for c, (_, cn) in enumerate(CC)],
              [("ht2", (b, a)), last], ("omm", (b, a)))
        op("vector", lambda e, bx: e.tensor_tensor(Y[:, a, :], MISC[k][:, 0:C], XB[:, a, :], ALU.add),
           need=[("omm", (b, a)), ("xb", b), ("store", b - 1)] + ([("ytt", (b - 1, 1))] if L0 else []), done=("y", (b, a)))
        free_after(k, ("y", (b, a)))
        if a == 1:
            op("sync", lambda e, bx: e.dma_start(y_nat[bx(b)].rearrange("(a q) c -> q a c", q=128), Y[:, :, :]),
               need=[("y", (b, 1))], done=("store", b), step=16)

    def y_transposed(b, a):
        k, last = misc()
        for c, (c0, cn) in enumerate(CC):
            op("tensor", lambda e, bx, c=c, c0=c0, cn=cn: e.transpose(MISC[k][0:cn, c * 128:(c + 1) * 128], Y[:, a, c0:c0 + cn], IDENT[:, :]),
               need=[("y", (b, a)), last], done=("ytt", (b, a)))
        op("scalar", lambda e, bx: e.copy(YT[0:106, :, a * 128:(a + 1) * 128], MISC[k][0:106, 0:384].rearrange("p (c q) -> p c q", c=3)),
           need=[("ytt", (b, a)), ("storet", b - 1)], done=("yt", (b, a)))
        op("scalar", lambda e, bx: e.copy(YT[96:107, 0:2, a * 128:(a + 1) * 128], MISC[k][96:107, 0:256].rearrange("p (c q) -> p c q", c=2)),
           need=[("yt", (b, a))], done=("yt2", (b, a)))
        free_after(k, ("yt2", (b, a)))
        if a == 1:
            for c, (c0, cn) in enumerate(CC):
                op("sync", lambda e, bx, c=c, c0=c0, cn=cn: e.dma_start(y_t[bx(b), c0:c0 + cn, :], YT[0:cn, c, :]),
                   need=[("yt2", (b, 1))], done=("storet", b), step=16)

    agenda = {}

    def at(slot, fn, *args):
        agenda.setdefault(slot, []).append((fn, args))

    for b in range(B):
        base = H * (b - 1)
        at(base - 8, loads, b)
        for m in range(3):
            at(base - 4 + 2 * m, project_q, b, m)
            at(base - 3 + 2 * m, project_k, b, m)
            at(base - 2 + 2 * m, split_rest, b, m)
        at(base + 2, spill_parts, b)
        at(base + 3, stack_parts, b)
        if L0:
            at(base, clear_text, b)
            at(base + 2, text_logits, b)
            at(base + 3, gram_text_ip, b)
            at(base + 4, project_v, b, 0)
            at(base + 5, probs_t, b)
            at(base + 6, sem_natural, b)
            at(base + 7, sem_transposed, b)
            at(base + 8, project_v, b, 1)
            at(base + 10, project_v, b, 2)
        else:
            at(base, ip_copies, b)
            at(base + 2, gram, b, 0)
            at(base + 3, gram, b, 1)
            at(base + 4, project_v, b, 0)
            at(base + 6, project_v, b, 1)
            at(base + 7, ip_norms, b)
            at(base + 8, ip_scores, b)
            at(base + 13, ip_values, b)
        base = H * b
        for s in range(base, base + H):
            at(s - LEAD, maxima, s)
            at(s, exponentials, s)
            if not L0:
                at(s + 1, quadratic, s)
        for hg in range(H // HG):
            g = b * (H // HG) + hg
            at(HG * g + HG - LEAD + 1, max_rows, g)
            at(HG * g + HG + 1, weighted_sums, g)
            at(HG * g + HG + 3, to_natural, g)
        base += H
        at(base - 4, load_residual, b)
        at(base + 2, residual, b)
        if L0:
            at(base + 5, combine_l0, b)
            at(base + 9, hs_t, b, 0)
            at(base + 11, hs_t, b, 1)
            at(base + 12, project_out, b, 0)
            at(base + 13, project_out, b, 1)
            at(base + 14, y_transposed, b, 0)
            at(base + 15, y_transposed, b, 1)
        else:
            at(base + 4, combine_l1, b, 0)
            at(base + 6, combine_l1, b, 1)
            at(base + 8, combine_l1, b, 2)
            at(base + 10, ip_probs_t, b)
            at(base + 11, ip_out, b, 0)
            at(base + 12, ip_out, b, 1)
            at(base + 13, hs_t, b, 0)
            at(base + 14, hs_t, b, 1)
            at(base + 15, project_out, b, 0)
            at(base + 16, project_out, b, 1)

    setup()
    rank = {maxima: 0, max_rows: 1, exponentials: 2, quadratic: 3, weighted_sums: 4, to_natural: 5}
    for slot in sorted(agenda):
        if slot >= 0 and slot % (2 * H) == 0:
            pl.start(slot // (2 * H))
        for fn, args in sorted(agenda[slot], key=lambda x: rank.get(x[0], 6)):
            fn(*args)
    pl.emit(nc, ctx)


def build(nc, a, out):
    x1 = nc.dram_tensor("x1", (B, S, C), F32, kind="Internal").ap()
    x1_t = nc.dram_tensor("x1_t", (B, C, S), F32, kind="Internal").ap()
    parts = nc.dram_tensor("qk_parts", (2, 2, 3, C, S), BF16, kind="Internal").ap()
    with ExitStack() as ctx:
        xattn_layer(nc, ctx, True, a["x"], a["x_t"], a["ctx_t"], a["mask"],
                    a["L0_xattn_Wq"], a["L0_xattn_Wk"], a["L0_xattn_Wv"], a["L0_xattn_Wk_ip"], a["L0_xattn_Wv_ip"],
                    a["L0_xattn_Wout"], a["bias0"], a["ident"], a["sel0"], None, a["ip_rows"], parts, x1, x1_t)
    with ExitStack() as ctx:
        xattn_layer(nc, ctx, False, x1, x1_t, a["ctx_t"], a["mask"],
                    a["L1_xattn_W_q"], a["L1_xattn_W_k"], a["L1_xattn_W_v"], a["L1_xattn_W_k_ip"], a["L1_xattn_W_v_ip"],
                    a["L1_xattn_W_out"], a["bias1"], a["ident"], a["sel1"], a["kmask"], a["vmask"], parts, out, None)


def kernel(**inputs):
    import numpy as np
    import ml_dtypes
    import concourse.bacc as _bacc
    from concourse.bass_utils import run_bass_kernel_spmd as _run

    arr = {k: np.ascontiguousarray(v) for k, v in inputs.items()}
    ctx2048 = arr.pop("ctx_2048")
    arr["x_t"] = np.ascontiguousarray(arr["x"].transpose(0, 2, 1))
    arr["ctx_t"] = np.ascontiguousarray(ctx2048.transpose(0, 2, 1))
    arr["bias0"] = np.ascontiguousarray(np.broadcast_to(arr.pop("L0_xattn_bout"), (128, C)))
    arr["bias1"] = np.ascontiguousarray(np.broadcast_to(arr.pop("L1_xattn_b_out"), (128, C)))
    arr["ident"] = np.eye(128, dtype=np.float32)
    for n, nt in ((0, 77), (1, T - 4)):
        s = np.zeros((4, H, T), np.float32)
        s[0::2, :, :nt] = 1
        if n == 0:
            s[1::2, :, nt:] = 1
        arr[f"sel{n}"] = s.astype(ml_dtypes.bfloat16)
    arr["ip_rows"] = np.repeat((np.arange(128) >= 77).astype(np.float32)[:, None], H, axis=1)
    arr["mask"] = np.ascontiguousarray(arr.pop("fside_S_0").reshape(2, 128).T)
    arr["kmask"] = np.ascontiguousarray(np.repeat((np.arange(128)[:, None] // D == np.arange(8)[None, :])
                                                  .astype(np.float32)[:, :, None], 4, axis=2))
    arr["vmask"] = (np.arange(80)[:, None] // 4 == np.arange(C)[None, :] // D).astype(np.float32)

    nc = _bacc.Bacc("TRN2", target_bir_lowering=False, num_devices=1)
    arrays, args = {}, {}
    for name, v in arr.items():
        arrays[f"in_{name}"] = v
        args[name] = nc.dram_tensor(f"in_{name}", v.shape, mybir.dt.from_np(v.dtype), kind="ExternalInput").ap()
    out = nc.dram_tensor("out_0", (B, S, C), F32, kind="ExternalOutput").ap()
    build(nc, args, out)
    r = _run(nc, [arrays], core_ids=[0])
    return r.results[0]["out_0"]
```

```python
from contextlib import ExitStack

import concourse.bass as bass
from concourse import mybir

F32 = mybir.dt.float32
F32R = mybir.dt.float32r
BF16 = mybir.dt.bfloat16
ALU = mybir.AluOpType
ACT = mybir.ActivationFunctionType
AX = mybir.AxisListType

B, S, C, CD, H, D = 16, 256, 320, 512, 20, 16
T = 256
HG = 4
SLOT = 32
CC = [(0, 107), (107, 107), (214, 106)]
MT = [(0, 128), (128, 128), (256, 64)]
KC = CD // 128
Q_PARTS = (0, 0, 0, 1, 1, 2)
K_PARTS = (0, 1, 2, 0, 1, 0)
KQ = 16 * len(Q_PARTS)
NATK = KQ
TRK = KQ + 4
LEAD = 11
SCALE = float(D) ** -0.5
EPS = 1e-12


class Plan:

    ENGINES = ("sync", "gpsimd", "scalar", "vector", "tensor")

    def __init__(self, per):
        self.ops = {e: [] for e in self.ENGINES}
        self.count, self.at, self.seen = {}, {}, {e: {} for e in self.ENGINES}
        self.period, self.per = -1, per
        self.starts = {}

    def start(self, period):
        self.period = period
        self.starts[period] = dict(self.count)

    def op(self, eng, fn, need=(), done=None, step=1):
        waits = []
        for label in need:
            if label is None:
                continue
            if label not in self.at:
                idx = label[1][0] if isinstance(label[1], tuple) else label[1]
                assert idx < 0, label
                continue
            kind, value = self.at[label]
            if self.seen[eng].get(kind, 0) < value:
                self.seen[eng][kind] = value
                waits.append((kind, value))
        if done is not None:
            kind, idx = done
            self.count[kind] = self.count.get(kind, 0) + step
            self.at[done] = (kind, self.count[kind])
            self.at[(kind.rstrip("01"), idx)] = (kind, self.count[kind])
            done = kind
        self.ops[eng].append((self.period, tuple(waits), fn, done, step))

    def same(self, p, q, grow):
        for e in self.ENGINES:
            a = [o for o in self.ops[e] if o[0] == p]
            b = [o for o in self.ops[e] if o[0] == q]
            if len(a) != len(b):
                return False
            for x, y in zip(a, b):
                if x[3] != y[3] or [w[0] for w in x[1]] != [w[0] for w in y[1]]:
                    return False
                if any(v + (q - p) * grow.get(k, 0) != w for (k, v), (_, w) in zip(x[1], y[1])):
                    return False
        return True

    def emit(self, nc, ctx):
        last = max(self.starts)
        first = None
        for f in range(1, last):
            grow = {k: self.starts[f + 1].get(k, 0) - self.starts[f].get(k, 0) for k in self.count}
            ends = [p for p in range(f + 1, last) if all(self.same(f, q, grow) for q in range(f + 1, p + 1))]
            if ends:
                first, end = f, ends[-1]
                break
        assert first is not None and end - first >= 4, (first, last)
        sems = {k: ctx.enter_context(nc.semaphore("s_" + k)) for k in self.count}
        gate = {k: ctx.enter_context(nc.semaphore("s_gate_" + k)) for k in ("sync", "gpsimd")}
        block = ctx.enter_context(nc.Block())

        def run(eng, period, i):
            for p, waits, fn, done, step in self.ops[eng[0]]:
                if p != period:
                    continue
                for k, v in waits:
                    eng[1].wait_ge(sems[k], v if i is None else v + i * grow[k])
                    if i is not None and eng[0] in ("sync", "gpsimd"):
                        eng[1].sem_inc(gate[eng[0]], 1)
                ins = fn(eng[1], (lambda b: b) if i is None else (lambda b: b + i * self.per))
                if done is not None:
                    ins.then_inc(sems[done], step)

        def program(name, e):
            for p in range(-1, first):
                run((name, e), p, None)
            if any(o[0] == first for o in self.ops[name]):
                with e.Fori(0, end - first + 1) as i:
                    run((name, e), first, i)
            for p in range(end + 1, last + 2):
                run((name, e), p, None)

        @block.sync
        def _(e):
            program("sync", e)
            for k, v in self.count.items():
                if k.startswith("store"):
                    e.wait_ge(sems[k], v)

        @block.gpsimd
        def _(e):
            program("gpsimd", e)

        @block.scalar
        def _(e):
            program("scalar", e)

        @block.vector
        def _(e):
            program("vector", e)

        @block.tensor
        def _(e):
            program("tensor", e)


def xattn_layer(nc, ctx, first_layer, x_nat, x_t, ctx_t, mask, wq, wk, wv, wki, wvi, wout, bias,
                ident_h, sel_h, kmask_h, vmask_h, parts_h, y_nat, y_t):
    NT = 77 if first_layer else T - 4
    NI = T - NT
    L0 = first_layer

    def sb(name, shape, dt=F32):
        return ctx.enter_context(nc.sbuf_tensor(name + ("_0" if L0 else "_1"), shape, dt))

    def bank(name):
        return ctx.enter_context(nc.psum_tensor(name + ("_0" if L0 else "_1"), [128, 512], F32))

    WQ = sb("WQ", [128, 3, C])
    WO = sb("WO", [128, 3, C])
    WK, WKI, WV, WVI = (sb(n, [128, KC, C]) for n in ("WK", "WKI", "WV", "WVI"))
    BIAS = sb("BIAS", [128, C])
    IDENT = sb("IDENT", [128, 128])
    MASK = sb("MASK", [128, 2])
    XT = sb("XT", [128, 2, 3, S])
    CT = sb("CT", [128, 2, KC, T])
    XN = sb("XN", [128, 2, 2, C])
    QKF = sb("QKF", [128, 3, 2 * S])
    RES = sb("RES", [128, 2 * S])
    PARTS = sb("PARTS", [128, 3, 3, 2 * S], BF16)
    QS = sb("QS", [TRK, 2, H, S], BF16)
    KS = sb("KS", [TRK, 2, H, T], BF16)
    MX = sb("MX", [128, 2, 2, 8])
    NH = sb("NH", [8, 2, 2, S], BF16)
    NP = 8
    P = sb("P", [128, NP, 2 * S])
    PVS = sb("PVS", [128, 2 * S])
    ON = sb("ON", [128, 2, 2 if L0 else 1, 2, H * SLOT])
    HS = sb("HS", [128, 2, C])
    HT = sb("HT", [128, 3, S])
    Y = sb("Y", [128, 2, C])
    XB = sb("XB", [128, 2, C])
    R1 = sb("R1", [128, 2, 2, H])
    VB = sb("VB", [128, 2, 2, H, SLOT])
    if L0:
        VA = sb("VA", [NT, 2, H, SLOT])
        CZ = sb("CZ", [128, KC, 128])
        IPONE = sb("IPONE", [128, H])
        G0 = sb("G0", [NT, T])
        TPM = sb("TPM", [128, 4, 2])
        TP = sb("TP", [128, 2, NT])
        TPN = sb("TPN", [128, 2, NT])
        TPT = sb("TPT", [NT, S])
        SN = sb("SN", [128, 2, 2, NI])
        ST = sb("ST", [128, 2, 2 * S])
        TMP = sb("TMP", [128, 2, 2, NI])
        TA = sb("TA", [128, 2, 2 * S])
        YT = sb("YT", [128, 3, S])
    else:
        GH = sb("GH", [128, 2, 4, 128], F32R)
        GL = sb("GL", [128, 2, 3, 128], F32R)
        NS = 4
        PH = sb("PH", [128, NS, 2 * S], F32R)
        PM = sb("PM", [128, NS, 2 * S])
        E21 = sb("E21", [128, SLOT])
        ONES = sb("ONES", [128, 128])
        ZP = sb("ZP", [128, 2, 2 * S])
        ZS = sb("ZS", [128, NP, S])
        SQ = sb("SQ", [128, KC, 4])
        CIP = sb("CIP", [128, KC, 80])
        RN = sb("RN", [128, 3, 4])
        RNI = sb("RNI", [128, 2, 4])
        KMASK = sb("KMASK", [128, 8, 4])
        KBD = sb("KBD", [128, 3, 8, 4])
        VMASK = sb("VMASK", [80, C])
        VIP = sb("VIP", [80, 2, C])
        SC = sb("SC", [128, 2, 2, 80])
        HALF = sb("HALF", [128, 2, H])
        NRM = sb("NRM", [128, 4, 2, H])
        FU = sb("FU", [128, 6, 2, 80])
        FM = sb("FM", [128, 4, 2, H])
        PT = sb("PT", [80, S])

    NAT = [bank(f"NAT{k}") for k in range(2)]
    TR = [bank(f"TR{k}") for k in range(2)]
    PV = bank("PV")
    n_misc = 3 if L0 else 2
    MISC = [bank(f"MISC{k}") for k in range(n_misc)]
    if not L0:
        GP = bank("GP")

    pl = Plan(2)
    op = pl.op
    qk_bank = {}
    misc_state = {"n": 0, "last": [None] * n_misc}

    def misc():
        k = misc_state["n"] % n_misc
        misc_state["n"] += 1
        return k, misc_state["last"][k]

    def free_after(k, label):
        misc_state["last"][k] = label

    def setup():
        n_w = 0
        def load(dst, src):
            op("sync", lambda e, bx: e.dma_start(dst, src), done=("w", 0), step=16)
        for c, (c0, cn) in enumerate(CC):
            load(WQ[0:cn, c, :], wq[c0:c0 + cn, :])
            load(WO[0:cn, c, :], wout[c0:c0 + cn, :])
        for w_sb, w_dr in ((WK, wk), (WKI, wki), (WV, wv), (WVI, wvi)):
            load(w_sb[:, :, :], w_dr.rearrange("(k p) n -> p k n", p=128))
        load(BIAS[:, :], bias)
        load(IDENT[:, :], ident_h)
        load(MASK[:, :], mask)
        for par in range(2):
            load(KS[KQ:TRK, par, :, :], sel_h)
        if not L0:
            load(KMASK[:, :, :], kmask_h)
            load(VMASK[:, :], vmask_h)
        ms = lambda ap, v: op("vector", lambda e, bx: e.memset(ap, v), done=("init", 0))
        ms(QS[KQ:TRK, :, :, :], 0.0)
        ms(VB[:, :, :, :, :], 0.0)
        if L0:
            ms(VA[:, :, :, :], 0.0)
            op("vector", lambda e, bx: e.memset(VA[:, :, :, D:D + 1], 1.0), need=[("init", 0)], done=("init", 0))
            ms(G0[:, :], 0.0)
            ms(CZ[:, :, :], 0.0)
            load(IPONE[:, :], vmask_h)
            op("vector", lambda e, bx: e.tensor_copy(VB[:, :, 0, :, D], IPONE[:, :].unsqueeze(1).broadcast_to([128, 2, H])),
               need=[("w", 0), ("init", 0)], done=("init", 0))
            op("vector", lambda e, bx: e.memset(VB[:, :, 1, :, D:D + 1], 1.0), need=[("init", 0)], done=("init", 0))
        else:
            ms(KS[0:KQ, :, :, NT:T], 0.0)
            ms(GH[:, :, :, :].bitcast(F32), 0.0)
            ms(GL[:, :, :, :].bitcast(F32), 0.0)
            ms(E21[:, :], 0.0)
            ms(ONES[:, :], 1.0)
            ms(HALF[:, :, :], 0.5)
            ms(KBD[:, :, :, :], 0.0)
            op("vector", lambda e, bx: e.memset(E21[:, 21:22], 1.0), need=[("init", 0)], done=("init", 0))
            op("vector", lambda e, bx: e.memset(VB[:, :, 0, :, D:D + 1], 1.0), done=("init", 0))
            op("vector", lambda e, bx: e.memset(VB[0:NT - 128, :, 1, :, D:D + 1], 1.0), done=("init", 0))
        op("tensor", lambda e, bx: e.transpose(MISC[0][:, 0:128], IDENT[:, :], IDENT[:, :]),
           need=[("w", 0), ("init", 0)], done=("warm", 0))

    READY = [("w", 0), ("init", 0)]

    def loads(b):
        p = b % 2
        for c, (c0, cn) in enumerate(CC):
            op("sync", lambda e, bx, c=c, c0=c0, cn=cn: e.dma_start(XT[0:cn, p, c, :], x_t[bx(b), c0:c0 + cn, :]),
               need=[("qk", (b - 2, 2))], done=(f"ld{p}", b), step=16)
        op("sync", lambda e, bx: e.dma_start(CT[:, p, :, :], ctx_t[bx(b)].rearrange("(k q) t -> q k t", q=128)),
           need=[("ctlast", b - 2), ("ctpool", b - 2)], done=(f"ld{p}", b), step=16)

    def load_residual(b):
        p = b % 2
        op("sync", lambda e, bx: e.dma_start(XN[:, p, :, :], x_nat[bx(b)].rearrange("(a q) c -> q a c", q=128)),
           need=[("xb", b - 2)], done=(f"xn{p}", b), step=16)

    def group(out, pairs, need, done=None):
        for n, (lhs, rhs) in enumerate(pairs):
            op("tensor", lambda e, bx, n=n, lhs=lhs, rhs=rhs: e.matmul(
                out, lhs, rhs, start=(n == 0), stop=(n == len(pairs) - 1)),
               need=need if n == 0 else (), done=done if n == len(pairs) - 1 else None)

    def project_q(b, m):
        p, (m0, mn) = b % 2, MT[m]
        qk_bank[m], last = misc()
        group(MISC[qk_bank[m]][0:mn, 0:S], [(WQ[0:cn, c, m0:m0 + mn], XT[0:cn, p, c, :]) for c, (_, cn) in enumerate(CC)],
              READY + [("ld", b), last])
        free_after(qk_bank[m], ("qkh", (b, m)))

    def project_k(b, m):
        p, (m0, mn), k = b % 2, MT[m], qk_bank[m]
        group(MISC[k][0:mn, S:S + NT], [(WK[:, c, m0:m0 + mn], CT[:, p, c, 0:NT]) for c in range(KC)], ())
        group(MISC[k][0:mn, S + NT:S + T], [(WKI[:, c, m0:m0 + mn], CT[:, p, c, NT:T]) for c in range(KC)], (),
              ("qk", (b, m)))
        op("scalar", lambda e, bx: e.copy(QKF[0:mn, m, :], MISC[k][0:mn, :]),
           need=[("qk", (b, m)), ("parts", (b - 1, m)), ("qkfread", b - 1)], done=("qkf", (b, m)))
        op("scalar", lambda e, bx: e.copy(PARTS[0:mn, m, 0, :], MISC[k][0:mn, :]),
           need=[("spill", b - 1)], done=("qkh", (b, m)))
        op("gpsimd", lambda e, bx: e.tensor_tensor(RES[0:mn, :], QKF[0:mn, m, :], PARTS[0:mn, m, 0, :], ALU.subtract),
           need=[("qkh", (b, m)), ("parts", (b, m - 1) if m else (b - 1, 2))], done=("split", (b, m)))

    def split_rest(b, m):
        mn = MT[m][1]
        op("scalar", lambda e, bx: e.copy(PARTS[0:mn, m, 1, :], RES[0:mn, :]), need=[("split", (b, m))], done=("split2", (b, m)))
        op("gpsimd", lambda e, bx: e.tensor_tensor(PARTS[0:mn, m, 2, :], RES[0:mn, :], PARTS[0:mn, m, 1, :], ALU.subtract),
           need=[("split2", (b, m))], done=("parts", (b, m)))

    def spill_parts(b):
        p = b % 2
        for m, (m0, mn) in enumerate(MT):
            for qk in range(2):
                op("sync", lambda e, bx, m=m, m0=m0, mn=mn, qk=qk: e.dma_start(
                    parts_h[p, qk, :, m0:m0 + mn, :].rearrange("j r t -> r j t"),
                    PARTS[0:mn, m, :, qk * S:(qk + 1) * S]),
                   need=[("parts", (b, m)), ("stack", b - 2)], done=("spill", b), step=16)

    def stack_parts(b):
        p = b % 2
        for r in range(len(Q_PARTS)):
            for qk, dst, parts, n in ((0, QS, Q_PARTS, S), (1, KS, K_PARTS, T if L0 else NT)):
                op("sync", lambda e, bx, r=r, qk=qk, dst=dst, parts=parts, n=n: e.dma_start(
                    dst[16 * r:16 * r + 16, p, :, 0:n],
                    parts_h[p, qk, parts[r], :, 0:n].rearrange("(h d) t -> d h t", d=D)),
                   need=[("spill", b), ("trans", 20 * (b - 2) + 19)] + READY, done=(f"stack{p}", b), step=16)

    def project_v(b, which):
        p = b % 2
        k, last = misc()
        tag = ("vmm", (b, which))
        need = READY + [("ld", b), last] + ([("cz", b)] if L0 else [])
        if L0:
            lhs, w, n, dst = {
                0: (lambda c: CT[:, p, c, 0:NT], WV, NT, VA[:, p, :, 0:D]),
                1: (lambda c: CZ[:, c, :], WVI, 128, VB[:, p, 0, :, 0:D]),
                2: (lambda c: CT[:, p, c, 128:T], WVI, 128, VB[:, p, 1, :, 0:D]),
            }[which]
        else:
            lhs, w, n, dst = {
                0: (lambda c: CT[:, p, c, 0:128], WV, 128, VB[:, p, 0, :, 0:D]),
                1: (lambda c: CT[:, p, c, 128:NT], WV, NT - 128, VB[0:NT - 128, p, 1, :, 0:D]),
            }[which]
        group(MISC[k][0:n, 0:C], [(lhs(c), w[:, c, :]) for c in range(KC)], need, tag)
        src = MISC[k][0:n, 0:C].rearrange("p (h d) -> p h d", d=D)
        op("scalar", lambda e, bx: e.copy(dst, src), need=[tag, ("pv", (b - 2, 4))] + READY, done=("v", b))
        pl.at[("vs", (b, which))] = pl.at[("v", b)]
        free_after(k, ("vs", (b, which)))
        if which == (2 if L0 else 1):
            pl.at[("ctlast", b)] = pl.at[tag]

    def clear_text(b):
        op("gpsimd", lambda e, bx: e.tensor_copy(CZ[:, :, NT:128], CT[:, b % 2, :, NT:128]),
           need=READY + [("ld", b), ("ctlast", b - 1)], done=("cz", b))
        pl.at[("ctpool", b)] = pl.at[("cz", b)]

    def text_logits(b):
        k, last = misc()
        for a in range(2):
            group(MISC[k][:, a * NT:(a + 1) * NT],
                  [(QKF[0:mn, m, a * 128:(a + 1) * 128], QKF[0:mn, m, S:S + NT]) for m, (_, mn) in enumerate(MT)],
                  [("qkf", (b, 2)), last], ("tl", b))
        pl.at[("qkfread", b)] = pl.at[("tl", b)]
        lg = MISC[k][:, 0:2 * NT].rearrange("p (a t) -> p a t", a=2)
        op("vector", lambda e, bx: e.tensor_reduce(TPM[:, 0, :], lg, AX.X, ALU.max, negate=True),
           need=[("tl", b), ("tpn", b - 1)], done=("tmax", b))
        op("vector", lambda e, bx: e.tensor_scalar(TPM[:, 1, :], TPM[:, 0, :], SCALE, None, ALU.mult),
           need=[("tmax", b), ("texp", b - 1)], done=("tbias", b))
        for a in range(2):
            op("scalar", lambda e, bx, a=a: e.activation(TP[:, a, :], MISC[k][:, a * NT:(a + 1) * NT], ACT.Exp,
                                                         bias=TPM[:, 1, a:a + 1], scale=SCALE,
                                                         accum_out=TPM[:, 2, a:a + 1]),
               need=[("tbias", b), ("tpn", b - 1)], done=("texp", b))
        free_after(k, ("texp", b))
        op("vector", lambda e, bx: e.reciprocal(TPM[:, 3, :], TPM[:, 2, :]), need=[("texp", b), ("tpn", b - 1)], done=("trz", b))
        op("vector", lambda e, bx: e.tensor_tensor(TPN[:, :, :], TP[:, :, :],
                                                   TPM[:, 3, :].unsqueeze(2).broadcast_to([128, 2, NT]), ALU.mult),
           need=[("trz", b), ("tpt", b - 1)], done=("tpn", b))

    def gram_text_ip(b):
        k, last = misc()
        group(MISC[k][0:NT, 0:NI], [(CT[:, b % 2, c, 0:NT], CT[:, b % 2, c, NT:T]) for c in range(KC)],
              READY + [("ld", b), last], ("g0", b))
        op("scalar", lambda e, bx: e.mul(G0[:, NT:T], MISC[k][0:NT, 0:NI], 0.5),
           need=[("g0", b), ("stmm", b - 1)] + READY, done=("g0s", b))
        free_after(k, ("g0s", b))

    def probs_t(b):
        k, last = misc()
        for a in range(2):
            op("tensor", lambda e, bx, a=a: e.transpose(MISC[k][0:NT, a * 128:(a + 1) * 128], TPN[:, a, :], IDENT[:, :]),
               need=[("tpn", b), last], done=("tpt", b))
        op("scalar", lambda e, bx: e.copy(TPT[:, :], MISC[k][0:NT, 0:S]), need=[("tpt", b), ("stmm", b - 1)], done=("tpts", b))
        free_after(k, ("tpts", b))

    def sem_natural(b):
        k, last = misc()
        for a in range(2):
            group(MISC[k][:, a * NI:(a + 1) * NI], [(TPT[:, a * 128:(a + 1) * 128], G0[:, NT:T])],
                  [("tpts", b), ("g0s", b), last], ("snmm", b))
        op("scalar", lambda e, bx: e.copy(SN[:, b % 2, :, :], MISC[k][:, 0:2 * NI].rearrange("p (a t) -> p a t", a=2)),
           need=[("snmm", b), ("max", 20 * (b - 2) + 19)], done=("sn", b))
        free_after(k, ("sn", b))

    def sem_transposed(b):
        k, last = misc()
        for a in range(2):
            group(MISC[k][:, a * S:(a + 1) * S], [(G0[:, a * 128:(a + 1) * 128], TPT[:, :])], [last], ("stmm", b))
        op("scalar", lambda e, bx: e.copy(ST[:, b % 2, :], MISC[k][:, :]),
           need=[("stmm", b), ("sadd", 20 * (b - 2) + 19)], done=("st", b))
        free_after(k, ("st", b))

    def gram(b, which):
        p = b % 2
        k, last = misc()
        need = READY + [("ld", b), last]
        if which == 0:
            group(MISC[k][:, 0:128], [(CT[:, p, c, 0:128], CT[:, p, c, 0:128]) for c in range(KC)], need)
            group(MISC[k][:, 128:132], [(CT[:, p, c, 0:128], CT[:, p, c, NT:T]) for c in range(KC)], (), ("gr", (b, 0)))
            jobs = [(0, slice(0, 128), MISC[k][:, 0:128])]
            n, c0, tt = 128, 128, 0
        else:
            n, c0, tt = NT - 128, NT, 1
            group(MISC[k][0:n, 0:T], [(CT[:, p, c, 128:NT], CT[:, p, c, :]) for c in range(KC)], need, ("gr", (b, 1)))
            jobs = [(1, slice(0, 128), MISC[k][0:n, 0:128]), (2, slice(0, n), MISC[k][0:n, 128:NT])]
        op("scalar", lambda e, bx: e.copy(VB[0:n, p, tt, :, D + 1:D + 5],
                                          MISC[k][0:n, c0:c0 + 4].unsqueeze(1).broadcast_to([n, H, 4])),
           need=[("gr", (b, which)), ("pv", (b - 2, 4))] + READY, done=("vc", b))
        for blk, cols, src in jobs:
            op("scalar", lambda e, bx, blk=blk, cols=cols, src=src: e.copy(GH[0:n, p, blk, cols], src),
               need=[("gpmm", 20 * (b - 2) + 19)], done=("gh", b))
        for blk, cols, src in jobs:
            op("vector", lambda e, bx, blk=blk, cols=cols, src=src: e.tensor_tensor(
                GL[0:n, p, blk, cols], src, GH[0:n, p, blk, cols].bitcast(F32), ALU.subtract),
               need=[("gh", b), ("gpmm", 20 * (b - 2) + 19)], done=("gl", b))
        pl.at[("gl", (b, which))] = pl.at[("gl", b)]
        free_after(k, ("gl", (b, which)))

    def gram_mirror(b):
        p, n = b % 2, NT - 128
        k, last = misc()
        op("tensor", lambda e, bx: e.transpose(MISC[k][:, 0:n], GH[0:n, p, 1, :].bitcast(F32), IDENT[0:n, 0:n]),
           need=[("gh", b), last], done=("g12", b))
        op("scalar", lambda e, bx: e.copy(GH[:, p, 3, 0:n], MISC[k][:, 0:n]),
           need=[("g12", b), ("gpmm", 20 * (b - 2) + 19)], done=("g12s", b))
        op("vector", lambda e, bx: e.tensor_scalar(GL[0:n, p, 1, :], GL[0:n, p, 1, :].bitcast(F32), 2.0, None, ALU.mult),
           need=[("gl", b)], done=("gl2", b))
        free_after(k, ("g12s", b))

    def ip_copies(b):
        p = b % 2
        ipc = CT[:, p, :, NT:T]
        op("gpsimd", lambda e, bx: e.tensor_tensor(SQ[:, :, :], ipc, ipc, ALU.mult),
           need=READY + [("ld", b), ("rnmm", b - 1)], done=("cip", b))
        op("gpsimd", lambda e, bx: e.tensor_copy(CIP[:, :, :].rearrange("p k (h n) -> p k h n", n=4),
                                                 ipc.unsqueeze(2).broadcast_to([128, KC, H, 4])),
           need=[("vipmm", b - 1)], done=("cip", b))
        pl.at[("ctpool", b)] = pl.at[("cip", b)]

    def ip_values(b):
        k, last = misc()
        group(MISC[k][0:80, 0:C], [(CIP[:, c, :], WVI[:, c, :]) for c in range(KC)], [("cip", b), last], ("vipmm", b))
        op("vector", lambda e, bx: e.tensor_tensor(VIP[:, b % 2, :], MISC[k][0:80, 0:C], VMASK[:, :], ALU.mult),
           need=READY + [("vipmm", b), ("ipmm", (b - 2, 1))], done=("vip", b))
        free_after(k, ("vip", b))

    def ip_norms(b):
        k, last = misc()
        group(MISC[k][:, 0:4], [(ONES[:, :], SQ[:, c, :]) for c in range(KC)], [("cip", b), last], ("rnmm", b))
        op("vector", lambda e, bx: e.tensor_copy(RN[:, 0, :], MISC[k][:, 0:4]), need=[("rnmm", b), ("rn", (b - 1, 1))], done=("rn", (b, 0)))
        free_after(k, ("rn", (b, 0)))
        op("gpsimd", lambda e, bx: e.tensor_tensor(RN[:, 1, :], RN[:, 0, :], HALF[:, 0, 0:4], ALU.pow),
           need=READY + [("rn", (b, 0)), ("rn", (b - 1, 2))], done=("rn1", b))

    def invert_ip_norms(b):
        op("vector", lambda e, bx: e.tensor_scalar(RN[:, 2, :], RN[:, 1, :], EPS, None, ALU.max),
           need=[("rn1", b), ("rn", (b - 1, 2))], done=("rn", (b, 1)))
        op("vector", lambda e, bx: e.reciprocal(RNI[:, b % 2, :], RN[:, 2, :]), need=[("rn", (b, 1)), ("fu", (b - 2, 0))], done=("rn", (b, 2)))

    def ip_keys(b):
        op("vector", lambda e, bx: e.tensor_tensor(
            KBD[:, 0:2, :, :], KMASK[:, :, :].unsqueeze(1).broadcast_to([128, 2, 8, 4]),
            QKF[:, 0:2, S + NT:S + T].unsqueeze(2).broadcast_to([128, 2, 8, 4]), ALU.mult),
           need=READY + [("qkf", (b, 2)), ("scmm", b - 1)], done=("kbd", b))
        op("vector", lambda e, bx: e.tensor_tensor(
            KBD[0:64, 2, :, :], KMASK[0:64, :, :], QKF[0:64, 2, S + NT:S + T].unsqueeze(1).broadcast_to([64, 8, 4]),
            ALU.mult), done=("kbd", b))

    def ip_scores(b):
        k, last = misc()
        for a in range(2):
            for m, (_, mn) in enumerate(MT):
                w = mn // 4
                group(MISC[k][:, a * 80 + m * 32:a * 80 + m * 32 + w],
                      [(QKF[0:mn, m, a * 128:(a + 1) * 128], KBD[0:mn, m, 0:w // 4, :])],
                      [("kbd", b), last], ("scmm", b))
        pl.at[("qkfread", b)] = pl.at[("scmm", b)]
        op("vector", lambda e, bx: e.tensor_scalar(SC[:, b % 2, :, :], MISC[k][:, 0:160].rearrange("p (a n) -> p a n", a=2),
                                                   SCALE, None, ALU.mult),
           need=[("scmm", b), ("fu", (b - 2, 1))], done=("sc", b))
        free_after(k, ("sc", b))

    def maxima(s):
        b, h = divmod(s, H)
        p, k, gp, j = b % 2, s % 2, (s // HG) % 2, h % HG
        for a in range(2):
            op("tensor", lambda e, bx, a=a: e.matmul(
                NAT[k][:, a * T:(a + 1) * T], QS[0:NATK, p, h, a * 128:(a + 1) * 128], KS[0:NATK, p, h, :],
                start=True, stop=True),
               need=READY + [("stack", b), ("max", s - 2)], done=("nat", s))
        v = NAT[k][:, :].rearrange("p (a t) -> p a t", a=2)
        op("vector", lambda e, bx: e.tensor_reduce(MX[:, gp, :, j], v[:, :, 0:NT], AX.X, ALU.max),
           need=[("nat", s), ("mxt", s // HG - 2)] + ([("sn", b), ("max", s - 2)] if L0 else []),
           done=None if L0 else ("max", s))
        if L0:
            for a in range(2):
                op("vector", lambda e, bx, a=a: e.tensor_tensor_reduce(
                    TMP[:, k, a, :], v[:, a, NT:T], SN[:, p, a, :], 1.0, -3.0e38, ALU.add, ALU.max,
                    MX[:, gp, a, HG + j:HG + j + 1]), done=("max", s))

    def max_rows(g):
        b, hg = divmod(g, H // HG)
        gp, p = g % 2, b % 2
        w = 8 if L0 else 4
        if L0:
            k, last = misc()
            rows = MISC[k][0:w, 0:S]
        else:
            rows, last = PV[0:w, S:2 * S], ("nm", g - 1)
        for a in range(2):
            op("tensor", lambda e, bx, a=a: e.transpose(rows[:, a * 128:(a + 1) * 128], MX[:, gp, a, 0:w], IDENT[:, :]),
               need=[("max", HG * g + HG - 1), last, None if L0 else ("pvs", g - 4)], done=("mxt", g))
        op("scalar", lambda e, bx: e.mul(NH[0:w, gp, 0, :], rows, -1.0),
           need=[("mxt", g), ("mrow", g - 2)], done=("nh", g))
        nh_rows["last"] = rows, (k if L0 else None)

    def max_rows_low(g):
        b, hg = divmod(g, H // HG)
        gp, p = g % 2, b % 2
        w = 8 if L0 else 4
        rows, k = nh_rows["last"]
        op("vector", lambda e, bx: e.scalar_tensor_tensor(NH[0:w, gp, 1, :], rows, -1.0, NH[0:w, gp, 0, :],
                                                          ALU.mult, ALU.subtract),
           need=[("nh", g)], done=("nm", g))
        if L0:
            free_after(k, ("nm", g))
        for part in range(2):
            for grp in range(w // HG):
                r = KQ + 2 * part + grp
                op("sync", lambda e, bx, part=part, grp=grp, r=r: e.dma_start(
                    QS[r:r + 1, p, HG * hg:HG * hg + HG, :], NH[HG * grp:HG * grp + HG, gp, part, :]),
                   need=READY + [("nm", g), ("trans", HG * (g - 10) + 3)], done=(f"mrow{gp}", g), step=16)

    nh_rows = {}

    def exponentials(s):
        b, h = divmod(s, H)
        p, k = b % 2, s % 2
        for a in range(2):
            op("tensor", lambda e, bx, a=a: e.matmul(
                TR[k][:, a * S:(a + 1) * S], KS[0:TRK, p, h, a * 128:(a + 1) * 128], QS[0:TRK, p, h, :],
                start=True, stop=True),
               need=READY + [("stack", b), ("mrow", s // HG), ("sadd" if L0 else "exp", s - 2)], done=("trans", s))
        if L0:
            op("vector", lambda e, bx: e.tensor_tensor(TA[:, k, :], TR[k][:, :], ST[:, p, :], ALU.add),
               need=[("trans", s), ("st", b), ("exp", s - 2)], done=("sadd", s))
        op("scalar", lambda e, bx: e.activation(P[:, s % NP, :], TA[:, k, :] if L0 else TR[k][:, :], ACT.Exp, scale=SCALE),
           need=[("sadd" if L0 else "trans", s), ("pv", divmod((s - NP) // HG, H // HG))],
           done=("exp", s))

    def split_exponentials(s):
        r, k = s % NP, s % NS
        op("scalar", lambda e, bx: e.copy(PH[:, k, :], P[:, r, :]), need=[("exp", s), ("gpmm", s - NS)], done=("ph", s))

    def multipliers(s):
        r, k = s % NP, s % NS
        op("vector", lambda e, bx: e.scalar_tensor_tensor(
            PM[:, k, :], P[:, r, :], 2.0, PH[:, k, :].bitcast(F32), ALU.mult, ALU.subtract),
           need=[("ph", s), ("zp", s - NS)], done=("pm", s))

    def quadratic(s):
        b, h = divmod(s, H)
        p, k = b % 2, s % NS
        n2 = NT - 128
        p0, p1 = PH[:, k, 0:S], PH[0:n2, k, S:2 * S]
        group(GP[:, 0:S], [(GH[:, p, 0, :], p0), (GL[:, p, 0, :], p0), (GH[0:n2, p, 1, :], p1), (GL[0:n2, p, 1, :], p1)],
              [("gl2", b), ("g12s", b),
               ("zp", s - 1) if s else ("ph", 0)])
        group(GP[:, S:2 * S], [(GH[:, p, 3, :], p0), (GH[0:n2, p, 2, :], p1), (GL[0:n2, p, 2, :], p1)], (), ("gpmm", s))
        op("vector", lambda e, bx: e.tensor_tensor(ZP[:, s % 2, :], GP[:, :], PM[:, k, :], ALU.mult),
           need=[("gpmm", s), ("pm", s), ("zs", s - 2)], done=("zp", s))
        op("gpsimd", lambda e, bx: e.tensor_tensor(ZS[:, s % NP, :], ZP[:, s % 2, 0:S], ZP[:, s % 2, S:2 * S], ALU.add),
           need=[("zp", s), ("pv", divmod((s - NP) // HG, H // HG))], done=("zs", s))

    def weighted_sums(g):
        b, hg = divmod(g, H // HG)
        p = b % 2
        lab = ("pv", (b, hg))
        need = [("exp", HG * g + HG - 1), ("v", b), ("pvs", g - 1)]
        if not L0:
            need.append(("nm", min(g + 3, B * H // HG - 1)))
        rounds = []
        if L0:
            rounds.append([(PV[SLOT * j:SLOT * (j + 1), 0:S], VA[:, p, HG * hg + j, :], P[0:NT, (HG * g + j) % NP, 0:S], True, True)
                           for j in range(HG)])
            for tt in range(2):
                rounds.append([(PV[SLOT * j:SLOT * (j + 1), S:2 * S], VB[:, p, tt, HG * hg + j, :],
                                P[:, (HG * g + j) % NP, tt * S:(tt + 1) * S], tt == 0, tt == 1) for j in range(HG)])
        else:
            need.append(("vc", b))
            need.append(("zs", HG * g + HG - 1))
            for tt in range(2):
                rounds.append([(PV[SLOT * j:SLOT * (j + 1), 0:S], VB[:, p, tt, HG * hg + j, :],
                                P[:, (HG * g + j) % NP, tt * S:(tt + 1) * S], tt == 0, False) for j in range(HG)])
            rounds.append([(PV[SLOT * j:SLOT * (j + 1), 0:S], E21[:, :], ZS[:, (HG * g + j) % NP, :], False, True)
                           for j in range(HG)])
        flat = [x for r in rounds for x in r]
        for n, (out, lhs, rhs, st, sp) in enumerate(flat):
            op("tensor", lambda e, bx, out=out, lhs=lhs, rhs=rhs, st=st, sp=sp: e.matmul(out, lhs, rhs, start=st, stop=sp),
               need=need if n == 0 else (), done=lab if n == len(flat) - 1 else None)
        w = 2 * S if L0 else S
        op("scalar", lambda e, bx: e.copy(PVS[:, 0:w], PV[:, 0:w]), need=[lab, ("ont", g - 1)], done=("pvs", g))

    def to_natural(g):
        b, hg = divmod(g, H // HG)
        k, last = misc()
        n = 4 if L0 else 2
        for a in range(n):
            op("tensor", lambda e, bx, a=a: e.transpose(MISC[k][:, a * 128:(a + 1) * 128], PVS[:, a * 128:(a + 1) * 128], IDENT[:, :]),
               need=[("pvs", g), last], done=("ont", g))
        op("scalar", lambda e, bx: e.copy(
            ON[:, b % 2, 0:n // 2, :, 128 * hg:128 * (hg + 1)],
            MISC[k][:, 0:n * 128].rearrange("p (v a n) -> p v a n", v=n // 2, a=2)),
           need=[("ont", g), ("hs", b - 2)], done=("on", g))
        free_after(k, ("on", g))

    def on_view(b, v):
        return ON[:, b % 2, v, :, :].rearrange("p a (h s) -> p a h s", s=SLOT)

    def residual(b):
        op("gpsimd", lambda e, bx: e.tensor_tensor(XB[:, :, :], XN[:, b % 2, :, :],
                                                   BIAS[:, :].unsqueeze(1).broadcast_to([128, 2, C]), ALU.add),
           need=READY + [("xn", b), ("y", (b - 1, 1))], done=("xb", b))

    HSV = HS[:, :, :].rearrange("p a (h d) -> p a h d", d=D)

    def combine_l0(b):
        A_, B_ = on_view(b, 0), on_view(b, 1)
        g = 5 * b + 4
        op("vector", lambda e, bx: e.reciprocal(R1[:, 0, :, :], A_[:, :, :, D]), need=[("on", g), ("hs", b - 1)], done=("cmb", (b, 0)))
        op("vector", lambda e, bx: e.reciprocal(R1[:, 1, :, :], B_[:, :, :, D]), done=("cmb", (b, 1)))
        for a in range(2):
            op("vector", lambda e, bx, a=a: e.tensor_scalar(R1[:, 1, a, :], R1[:, 1, a, :], MASK[:, a:a + 1], None, ALU.mult),
               need=READY + [("cmb", (b, 1))], done=("cmb", (b, 2)))
        bc = lambda v: R1[:, v, :, :].unsqueeze(3).broadcast_to([128, 2, H, D])
        for v, X in enumerate((A_, B_)):
            op("gpsimd", lambda e, bx, v=v, X=X: e.tensor_tensor(X[:, :, :, 0:D], X[:, :, :, 0:D], bc(v), ALU.mult),
               need=[("cmb", (b, 2))], done=("cmb", (b, 3)))
        op("gpsimd", lambda e, bx: e.tensor_tensor(HSV, A_[:, :, :, 0:D], B_[:, :, :, 0:D], ALU.add),
           need=[("cmb", (b, 3)), ("hst", (b - 1, 1))], done=("hs", b))

    def combine_l1(b, stage):
        A_ = on_view(b, 0)
        g = 5 * b + 4
        V = lambda fn, need=(), done=None: op("vector", fn, need=need, done=done) if stage == now[0] else None
        q = b % 2
        now = [0]
        rz = R1[:, 0, :, :]
        V(lambda e, bx: e.reciprocal(rz, A_[:, :, :, D]), [("on", g), ("hs", b - 1), ("fu", (b - 1, 0))], ("cmb", (b, 0)))
        V(lambda e, bx: e.tensor_scalar(NRM[:, 0, :, :], A_[:, :, :, D + 5], 0.0, None, ALU.max), [("nrm", b - 1)], ("cmb", (b, 1)))
        if stage == 0:
          op("gpsimd", lambda e, bx: e.tensor_tensor(NRM[:, 1, :, :], NRM[:, 0, :, :], HALF[:, :, :], ALU.pow),
           need=READY + [("cmb", (b, 1)), ("cmb", (b - 1, 2))], done=("nrm", b))
        now[0] = 1
        V(lambda e, bx: e.tensor_tensor(NRM[:, 2, :, :], NRM[:, 1, :, :], rz, ALU.mult), [("nrm", b), ("cmb", (b - 1, 3))], ("cmb", (b, 2)))
        V(lambda e, bx: e.tensor_scalar(NRM[:, 2, :, :], NRM[:, 2, :, :], EPS, None, ALU.max), [("cmb", (b, 2))], ("cmb", (b, 3)))
        V(lambda e, bx: e.reciprocal(NRM[:, 3, :, :], NRM[:, 2, :, :]), [("cmb", (b, 3)), ("cmb", (b - 1, 5))], ("cmb", (b, 4)))
        V(lambda e, bx: e.scalar_tensor_tensor(NRM[:, 3, :, :], NRM[:, 3, :, :], 0.5, rz, ALU.mult, ALU.mult), [("cmb", (b, 4))], ("cmb", (b, 5)))
        F = lambda i: FU[:, i, :, :].rearrange("p a (h n) -> p a h n", n=4)
        V(lambda e, bx: e.tensor_tensor(F(0), A_[:, :, :, D + 1:D + 5], NRM[:, 3, :, :].unsqueeze(3).broadcast_to([128, 2, H, 4]), ALU.mult),
          [("cmb", (b, 5)), ("fu", (b - 1, 0))], ("f1", b))
        V(lambda e, bx: e.tensor_tensor(FU[:, 1, :, :].rearrange("p a (h n) -> p (a h) n", n=4),
                                        FU[:, 0, :, :].rearrange("p a (h n) -> p (a h) n", n=4),
                                        RNI[:, q, :].unsqueeze(1).broadcast_to([128, 2 * H, 4]), ALU.mult),
          [("f1", b), ("rn", (b, 2)), ("fu", (b - 1, 1))], ("fu", (b, 0)))
        V(lambda e, bx: e.tensor_tensor(FU[:, 2, :, :], FU[:, 1, :, :], SC[:, q, :, :], ALU.add), [("fu", (b, 0)), ("sc", b), ("fu", (b - 1, 2))], ("fu", (b, 1)))
        V(lambda e, bx: e.tensor_reduce(FM[:, 0, :, :], F(2), AX.X, ALU.max), [("fu", (b, 1)), ("fu", (b - 1, 2))], ("f2", b))
        V(lambda e, bx: e.tensor_tensor(F(3), F(2), FM[:, 0, :, :].unsqueeze(3).broadcast_to([128, 2, H, 4]), ALU.subtract),
          [("f2", b), ("fexp", b - 1)], ("fu", (b, 2)))
        if stage == 1:
          op("scalar", lambda e, bx: e.activation(FU[:, 4, :, :], FU[:, 3, :, :], ACT.Exp), need=[("fu", (b, 2)), ("fu", (b - 1, 4))], done=("fexp", b))
        now[0] = 2
        V(lambda e, bx: e.tensor_reduce(FM[:, 1, :, :], F(4), AX.X, ALU.add), [("fexp", b), ("fu", (b - 1, 3))], ("f3", b))
        V(lambda e, bx: e.reciprocal(FM[:, 2, :, :], FM[:, 1, :, :]), [("f3", b), ("fu", (b - 1, 3))], ("f4", b))
        for a in range(2):
            V(lambda e, bx, a=a: e.tensor_scalar(FM[:, 3, a, :], FM[:, 2, a, :], MASK[:, a:a + 1], None, ALU.mult),
              READY + [("f4", b), ("fu", (b - 1, 4))], ("fu", (b, 3)))
        V(lambda e, bx: e.tensor_tensor(F(5), F(4), FM[:, 3, :, :].unsqueeze(3).broadcast_to([128, 2, H, 4]), ALU.mult),
          [("fu", (b, 3)), ("ptt", b - 1)], ("fu", (b, 4)))
        V(lambda e, bx: e.tensor_tensor(HSV, A_[:, :, :, 0:D], rz.unsqueeze(3).broadcast_to([128, 2, H, D]), ALU.mult),
          [("hst", (b - 1, 1))], ("tx", b))

    def ip_probs_t(b):
        k, last = misc()
        for a in range(2):
            op("tensor", lambda e, bx, a=a: e.transpose(MISC[k][0:80, a * 128:(a + 1) * 128], FU[:, 5, a, :], IDENT[:, :]),
               need=[("fu", (b, 4)), last], done=("ptt", b))
        op("scalar", lambda e, bx: e.copy(PT[:, :], MISC[k][0:80, 0:S]), need=[("ptt", b), ("ipmm", (b - 1, 1))], done=("pt", b))
        free_after(k, ("pt", b))

    def ip_out(b, a):
        k, last = misc()
        group(MISC[k][:, 0:C], [(PT[:, a * 128:(a + 1) * 128], VIP[:, b % 2, :])], [("pt", b), ("vip", b), last], ("ipmm", (b, a)))
        op("vector", lambda e, bx: e.tensor_tensor(HS[:, a, :], HS[:, a, :], MISC[k][:, 0:C], ALU.add),
           need=[("ipmm", (b, a)), ("tx", b)], done=("hs", b))
        pl.at[("hsa", (b, a))] = pl.at[("hs", b)]
        free_after(k, ("hsa", (b, a)))

    def hs_t(b, a):
        k, last = misc()
        for c, (c0, cn) in enumerate(CC):
            op("tensor", lambda e, bx, c=c, c0=c0, cn=cn: e.transpose(MISC[k][0:cn, c * 128:(c + 1) * 128], HS[:, a, c0:c0 + cn], IDENT[:, :]),
               need=[("hs", b), last], done=("hst", (b, a)))
        src = MISC[k][0:106, 0:384].rearrange("p (c q) -> p c q", c=3)
        op("scalar", lambda e, bx: e.copy(HT[0:106, :, a * 128:(a + 1) * 128], src),
           need=[("hst", (b, a)), ("omm", (b - 1, 1))], done=("ht", (b, a)))
        op("scalar", lambda e, bx: e.copy(HT[96:107, 0:2, a * 128:(a + 1) * 128],
                                          MISC[k][96:107, 0:256].rearrange("p (c q) -> p c q", c=2)),
           need=[("ht", (b, a))], done=("ht2", (b, a)))
        free_after(k, ("ht2", (b, a)))

    def project_out(b, a):
        k, last = misc()
        group(MISC[k][:, 0:C], [(HT[0:cn, c, a * 128:(a + 1) * 128], WO[0:cn, c, :]) for c, (_, cn) in enumerate(CC)],
              [("ht2", (b, a)), last], ("omm", (b, a)))
        op("vector", lambda e, bx: e.tensor_tensor(Y[:, a, :], MISC[k][:, 0:C], XB[:, a, :], ALU.add),
           need=[("omm", (b, a)), ("xb", b), ("store", b - 1)] + ([("ytt", (b - 1, 1))] if L0 else []), done=("y", (b, a)))
        free_after(k, ("y", (b, a)))
        if a == 1:
            op("sync", lambda e, bx: e.dma_start(y_nat[bx(b)].rearrange("(a q) c -> q a c", q=128), Y[:, :, :]),
               need=[("y", (b, 1))], done=("store", b), step=16)

    def y_transposed(b, a):
        k, last = misc()
        for c, (c0, cn) in enumerate(CC):
            op("tensor", lambda e, bx, c=c, c0=c0, cn=cn: e.transpose(MISC[k][0:cn, c * 128:(c + 1) * 128], Y[:, a, c0:c0 + cn], IDENT[:, :]),
               need=[("y", (b, a)), last], done=("ytt", (b, a)))
        op("scalar", lambda e, bx: e.copy(YT[0:106, :, a * 128:(a + 1) * 128], MISC[k][0:106, 0:384].rearrange("p (c q) -> p c q", c=3)),
           need=[("ytt", (b, a)), ("storet", b - 1)], done=("yt", (b, a)))
        op("scalar", lambda e, bx: e.copy(YT[96:107, 0:2, a * 128:(a + 1) * 128], MISC[k][96:107, 0:256].rearrange("p (c q) -> p c q", c=2)),
           need=[("yt", (b, a))], done=("yt2", (b, a)))
        free_after(k, ("yt2", (b, a)))
        if a == 1:
            for c, (c0, cn) in enumerate(CC):
                op("sync", lambda e, bx, c=c, c0=c0, cn=cn: e.dma_start(y_t[bx(b), c0:c0 + cn, :], YT[0:cn, c, :]),
                   need=[("yt2", (b, 1))], done=("storet", b), step=16)

    agenda = {}

    def at(slot, fn, *args):
        agenda.setdefault(slot, []).append((fn, args))

    for b in range(B):
        base = H * (b - 1)
        at(base - 13, loads, b)
        for m, (q, k) in enumerate(((-6, -5), (-4, -2), (-1, 0)) if L0 else ((-10, -8), (-4, -3), (-2, 0))):
            at(base + q, project_q, b, m)
            at(base + k, project_k, b, m)
            at(base + k + 1, split_rest, b, m)
        at(base + 1, spill_parts, b)
        at(base + 2, stack_parts, b)
        if L0:
            at(base, clear_text, b)
            at(base + 2, text_logits, b)
            at(base + 3, gram_text_ip, b)
            at(base + 4, project_v, b, 0)
            at(base + 5, probs_t, b)
            at(base + 6, sem_natural, b)
            at(base + 6, sem_transposed, b)
            at(base + 8, project_v, b, 1)
            at(base + 10, project_v, b, 2)
        else:
            at(base, ip_copies, b)
            at(base + 4, gram, b, 0)
            at(base + 5, gram, b, 1)
            at(base + 6, project_v, b, 0)
            at(base + 7, gram_mirror, b)
            at(base + 8, project_v, b, 1)
            at(base + 8, ip_keys, b)
            at(base + 8, ip_norms, b)
            at(base + 11, invert_ip_norms, b)
            at(base + 11, ip_scores, b)
            at(base + 14, ip_values, b)
        base = H * b
        for s in range(base, base + H):
            at(s - LEAD, maxima, s)
            at(s, exponentials, s)
            if not L0:
                at(s, split_exponentials, s)
                at(s + 1, multipliers, s)
                at(s + 2, quadratic, s)
        for hg in range(H // HG):
            g = b * (H // HG) + hg
            at(HG * g + HG - LEAD + 1, max_rows, g)
            at(HG * g + HG - LEAD + 1, max_rows_low, g)
            at(HG * g + HG + (1 if L0 else 3), weighted_sums, g)
            at(HG * g + HG + (3 if L0 else 5), to_natural, g)
        base += H
        at(base - 4, load_residual, b)
        at(base + (2 if L0 else 3), residual, b)
        if L0:
            at(base + 4, combine_l0, b)
            at(base + 7, hs_t, b, 0)
            at(base + 7, hs_t, b, 1)
            at(base + 11, project_out, b, 0)
            at(base + 12, project_out, b, 1)
            at(base + 14, y_transposed, b, 0)
            at(base + 15, y_transposed, b, 1)
        else:
            at(base + 7, combine_l1, b, 0)
            at(base + 10, combine_l1, b, 1)
            at(base + 11, combine_l1, b, 2)
            at(base + 12, ip_probs_t, b)
            at(base + 13, ip_out, b, 0)
            at(base + 13, ip_out, b, 1)
            at(base + 14, hs_t, b, 0)
            at(base + 14, hs_t, b, 1)
            at(base + 21, project_out, b, 0)
            at(base + 22, project_out, b, 1)

    setup()
    rank = {maxima: 0, max_rows: 1, exponentials: 2, split_exponentials: 2, multipliers: 1.5, quadratic: 3, weighted_sums: 4, to_natural: 5, project_k: 4.5, max_rows_low: 3.5}
    for slot in sorted(agenda):
        if slot >= 0 and slot % (2 * H) == 0:
            pl.start(slot // (2 * H))
        for fn, args in sorted(agenda[slot], key=lambda x: rank.get(x[0], 6)):
            fn(*args)
    assert misc_state["n"] // B * 2 % n_misc == 0 and 2 * H % NP == 0
    pl.emit(nc, ctx)


def build(nc, a, out):
    x1 = nc.dram_tensor("x1", (B, S, C), F32, kind="Internal").ap()
    x1_t = nc.dram_tensor("x1_t", (B, C, S), F32, kind="Internal").ap()
    parts = nc.dram_tensor("qk_parts", (2, 2, 3, C, S), BF16, kind="Internal").ap()
    with ExitStack() as ctx:
        xattn_layer(nc, ctx, True, a["x"], a["x_t"], a["ctx_t"], a["mask"],
                    a["L0_xattn_Wq"], a["L0_xattn_Wk"], a["L0_xattn_Wv"], a["L0_xattn_Wk_ip"], a["L0_xattn_Wv_ip"],
                    a["L0_xattn_Wout"], a["bias0"], a["ident"], a["sel0"], None, a["ip_rows"], parts, x1, x1_t)
    with ExitStack() as ctx:
        xattn_layer(nc, ctx, False, x1, x1_t, a["ctx_t"], a["mask"],
                    a["L1_xattn_W_q"], a["L1_xattn_W_k"], a["L1_xattn_W_v"], a["L1_xattn_W_k_ip"], a["L1_xattn_W_v_ip"],
                    a["L1_xattn_W_out"], a["bias1"], a["ident"], a["sel1"], a["kmask"], a["vmask"], parts, out, None)


def kernel(**inputs):
    import numpy as np
    import ml_dtypes
    import concourse.bacc as _bacc
    from concourse.bass_utils import run_bass_kernel_spmd as _run

    arr = {k: np.ascontiguousarray(v) for k, v in inputs.items()}
    ctx2048 = arr.pop("ctx_2048")
    arr["x_t"] = np.ascontiguousarray(arr["x"].transpose(0, 2, 1))
    arr["ctx_t"] = np.ascontiguousarray(ctx2048.transpose(0, 2, 1))
    arr["bias0"] = np.ascontiguousarray(np.broadcast_to(arr.pop("L0_xattn_bout"), (128, C)))
    arr["bias1"] = np.ascontiguousarray(np.broadcast_to(arr.pop("L1_xattn_b_out"), (128, C)))
    arr["ident"] = np.eye(128, dtype=np.float32)
    for n, nt in ((0, 77), (1, T - 4)):
        s = np.zeros((4, H, T), np.float32)
        s[0::2, :, :nt] = 1
        if n == 0:
            s[1::2, :, nt:] = 1
        arr[f"sel{n}"] = s.astype(ml_dtypes.bfloat16)
    arr["ip_rows"] = np.repeat((np.arange(128) >= 77).astype(np.float32)[:, None], H, axis=1)
    arr["mask"] = np.ascontiguousarray(arr.pop("fside_S_0").reshape(2, 128).T)
    arr["kmask"] = np.ascontiguousarray(np.repeat((np.arange(128)[:, None] // D == np.arange(8)[None, :])
                                                  .astype(np.float32)[:, :, None], 4, axis=2))
    arr["vmask"] = (np.arange(80)[:, None] // 4 == np.arange(C)[None, :] // D).astype(np.float32)

    nc = _bacc.Bacc("TRN2", target_bir_lowering=False, num_devices=1)
    arrays, args = {}, {}
    for name, v in arr.items():
        arrays[f"in_{name}"] = v
        args[name] = nc.dram_tensor(f"in_{name}", v.shape, mybir.dt.from_np(v.dtype), kind="ExternalInput").ap()
    out = nc.dram_tensor("out_0", (B, S, C), F32, kind="ExternalOutput").ap()
    build(nc, args, out)
    r = _run(nc, [arrays], core_ids=[0])
    return r.results[0]["out_0"]
```

```python
from contextlib import ExitStack

import concourse.bass as bass
from concourse import mybir

F32 = mybir.dt.float32
F32R = mybir.dt.float32r
BF16 = mybir.dt.bfloat16
ALU = mybir.AluOpType
ACT = mybir.ActivationFunctionType
AX = mybir.AxisListType

B, S, C, CD, H, D = 16, 256, 320, 512, 20, 16
T = 256
HG = 4
SLOT = 32
CK, CC = 107, (0, 107, 213)
MT = [(0, 128), (128, 128), (256, 64)]
KC = CD // 128
Q_PARTS = (0, 0, 0, 1, 1, 2)
K_PARTS = (0, 1, 2, 0, 1, 0)
KQ = D * len(Q_PARTS)
LEAD = 11
SCALE = float(D) ** -0.5
EPS = 1e-12


class Plan:

    ENGINES = ("sync", "gpsimd", "scalar", "vector", "tensor")

    def __init__(self, per):
        self.ops = {e: [] for e in self.ENGINES}
        self.count, self.at, self.seen = {}, {}, {e: {} for e in self.ENGINES}
        self.period, self.per = -1, per
        self.starts = {}

    def start(self, period):
        self.period = period
        self.starts[period] = dict(self.count)

    def op(self, eng, fn, need=(), done=None, step=1):
        waits = []
        for label in need:
            if label is None:
                continue
            if label not in self.at:
                idx = label[1][0] if isinstance(label[1], tuple) else label[1]
                assert idx < 0, label
                continue
            kind, value = self.at[label]
            if self.seen[eng].get(kind, 0) < value:
                self.seen[eng][kind] = value
                waits.append((kind, value))
        if done is not None:
            kind, idx = done
            self.count[kind] = self.count.get(kind, 0) + step
            self.at[done] = (kind, self.count[kind])
            self.at[(kind.rstrip("01"), idx)] = (kind, self.count[kind])
            done = kind
        self.ops[eng].append((self.period, tuple(waits), fn, done, step))

    def same(self, p, q, grow):
        for e in self.ENGINES:
            a = [o for o in self.ops[e] if o[0] == p]
            b = [o for o in self.ops[e] if o[0] == q]
            if len(a) != len(b):
                return False
            for x, y in zip(a, b):
                if x[3] != y[3] or [w[0] for w in x[1]] != [w[0] for w in y[1]]:
                    return False
                if any(v + (q - p) * grow.get(k, 0) != w for (k, v), (_, w) in zip(x[1], y[1])):
                    return False
        return True

    def emit(self, nc, ctx, gate):
        last = max(self.starts)
        first = None
        for f in range(1, last):
            grow = {k: self.starts[f + 1].get(k, 0) - self.starts[f].get(k, 0) for k in self.count}
            ends = [p for p in range(f + 1, last) if all(self.same(f, q, grow) for q in range(f + 1, p + 1))]
            if ends:
                first, end = f, ends[-1]
                break
        assert first is not None and end - first >= 4, (first, last)
        sems = {k: ctx.enter_context(nc.semaphore("s_" + k)) for k in self.count}
        block = ctx.enter_context(nc.Block())

        def run(eng, period, i):
            for p, waits, fn, done, step in self.ops[eng[0]]:
                if p != period:
                    continue
                for k, v in waits:
                    eng[1].wait_ge(sems[k], v if i is None else v + i * grow[k])
                    if i is not None and eng[0] in ("sync", "gpsimd"):
                        eng[1].sem_inc(gate[eng[0]], 1)
                ins = fn(eng[1], (lambda b: b) if i is None else (lambda b: b + i * self.per))
                if done is not None:
                    ins.then_inc(sems[done], step)

        def program(name, e):
            for p in range(-1, first):
                run((name, e), p, None)
            if any(o[0] == first for o in self.ops[name]):
                with e.Fori(0, end - first + 1) as i:
                    run((name, e), first, i)
            for p in range(end + 1, last + 2):
                run((name, e), p, None)

        @block.sync
        def _(e):
            program("sync", e)
            for k, v in self.count.items():
                if k.startswith("store"):
                    e.wait_ge(sems[k], v)

        @block.gpsimd
        def _(e):
            program("gpsimd", e)

        @block.scalar
        def _(e):
            program("scalar", e)

        @block.vector
        def _(e):
            program("vector", e)

        @block.tensor
        def _(e):
            program("tensor", e)


def xattn_layer(nc, ctx, gate, first_layer, x_nat, x_t, ctx_t, mask, wq, wk, wv, wki, wvi, wout, bias,
                ident_h, sel_h, kmask_h, vmask_h, parts_h, y_nat, y_t):
    NT = 77 if first_layer else T - 4
    NI = T - NT
    L0 = first_layer
    NG = 2 if L0 else 1
    TRK = KQ + 2 * NG

    def sb(name, shape, dt=F32):
        return ctx.enter_context(nc.sbuf_tensor(name + ("_0" if L0 else "_1"), shape, dt))

    def bank(name):
        return ctx.enter_context(nc.psum_tensor(name + ("_0" if L0 else "_1"), [128, 512], F32))

    pair = lambda name, shape: (sb(name + "H", shape, F32R), sb(name + "L", shape, F32R))
    WQ, WO = pair("WQ", [128, 3, C]), pair("WO", [128, 3, C])
    WK, WKI = (sb(n, [128, KC, C]) for n in ("WK", "WKI"))
    WV, WVI = ((pair if L0 else sb)(n, [128, KC, C]) for n in ("WV", "WVI"))
    BIAS = sb("BIAS", [128, C])
    IDENT = sb("IDENT", [128, 128])
    MASK = sb("MASK", [128, 2])
    XT, XTS = sb("XT", [128, 3, S]), pair("XTS", [128, 3, S])
    CT = sb("CT", [128, KC, T])
    QKF = sb("QKF", [128, 3, 2 * S])
    RES = sb("RES", [128, 2 * S])
    PARTS = sb("PARTS", [128, 3, 3, 2 * S], BF16)
    QS = sb("QS", [TRK, 2, H, S], BF16)
    KS = sb("KS", [TRK, 2, H, T], BF16)
    MX = sb("MX", [128, 2, 2, 8])
    NH = sb("NH", [8, 2, 2, S], BF16)
    NP = 8
    P = sb("P", [128, NP, 2 * S])
    PVS = sb("PVS", [128, 2 * S if L0 else S])
    NV = D + 1 if L0 else D + 6
    ON = sb("ON", [128, 2, 2 if L0 else 1, 2, H * NV])
    HS = sb("HS", [128, 2, C])
    HT = pair("HT", [128, 3, S])
    Y = sb("Y", [128, 2, C])
    XB = sb("XB", [128, 2, C])
    R1 = sb("R1", [128, 2, 2, H])
    VB = sb("VB", [128, 2, 2, H, SLOT])
    if L0:
        CTS = pair("CTS", [128, KC, T])
        VA = sb("VA", [NT, 2, H, SLOT])
        CZ = pair("CZ", [128, KC, 128])
        IPONE = sb("IPONE", [128, H])
        G0 = sb("G0", [NT, T])
        TPM = sb("TPM", [128, 4, 2])
        TP = sb("TP", [128, 2, NT])
        TPT = sb("TPT", [NT, S])
        SN = sb("SN", [128, 2, 2, NI])
        ST = sb("ST", [128, 2, 2 * S])
        TMP = sb("TMP", [128, 2, 2, NI])
        TA = sb("TA", [128, 2, 2 * S])
        YT = sb("YT", [128, 3, S])
    else:
        GH = sb("GH", [128, 2, 4, 128], F32R)
        GL = sb("GL", [128, 2, 3, 128], F32R)
        NS = 4
        PH = sb("PH", [128, NS, 2 * S], F32R)
        PM = sb("PM", [128, NS, 2 * S])
        E21 = sb("E21", [128, SLOT])
        ONES = sb("ONES", [128, 128])
        ZP = sb("ZP", [128, 2, 2 * S])
        ZS = sb("ZS", [128, NP, S])
        SQ = sb("SQ", [128, KC, 4])
        CIP = sb("CIP", [128, KC, 80])
        RN = sb("RN", [128, 3, 4])
        RNI = sb("RNI", [128, 2, 4])
        KMASK = sb("KMASK", [128, 8, 4])
        KBD = sb("KBD", [128, 3, 8, 4])
        VMASK = sb("VMASK", [80, C])
        VIP = sb("VIP", [80, 2, C])
        SC = sb("SC", [128, 2, 2, 80])
        HALF = sb("HALF", [128, 2, H])
        NRM = sb("NRM", [128, 4, 2, H])
        FU = sb("FU", [128, 6, 2, 80])
        FM = sb("FM", [128, 4, 2, H])
        PT = sb("PT", [80, S])

    NAT = [bank(f"NAT{k}") for k in range(2)]
    TR = [bank(f"TR{k}") for k in range(2)]
    PV = bank("PV")
    n_misc = 3 if L0 else 2
    MISC = [bank(f"MISC{k}") for k in range(n_misc)]
    if not L0:
        GP = bank("GP")

    pl = Plan(2)
    op = pl.op
    qk_bank = {}
    misc_state = {"n": 0, "last": [None] * n_misc}

    def misc():
        k = misc_state["n"] % n_misc
        misc_state["n"] += 1
        return k, misc_state["last"][k]

    def free_after(k, label):
        misc_state["last"][k] = label

    def split_pair(name, idx, dst, src, need, done, eng="gpsimd"):
        hi, lo = dst
        op("scalar", lambda e, bx: e.copy(hi, src), need=need, done=(name, idx))
        op(eng, lambda e, bx: e.tensor_tensor(lo, src, hi.bitcast(F32), ALU.subtract), need=[(name, idx)], done=done)

    def setup():
        def load(group, dst, src):
            op("sync", lambda e, bx: e.dma_start(dst, src), done=(group, 0), step=16)
        def load_rows(group, dst, src):
            for c, c0 in enumerate(CC):
                skip = c // 2
                load(group, dst[skip:CK, c, :], src[c0 + skip:c0 + CK, :])
        whole = lambda w_dr: w_dr.rearrange("(k p) n -> p k n", p=128)
        flat = P[:, :, :].rearrange("p r n -> p (r n)")
        stage = lambda n0, k: flat[:, n0:n0 + k * C].rearrange("p (k n) -> p k n", n=C)
        q_raw, vi_raw, v_raw = stage(0, 3), stage(3 * C, KC), stage((3 + KC) * C, KC)
        o_raw = (TA if L0 else PM)[:, :, :].rearrange("p r n -> p (r n)")[:, 0:3 * C].rearrange("p (k n) -> p k n", n=C)
        op("vector", lambda e, bx: e.memset(q_raw[0:1, 2, :], 0.0), done=("init", 0))
        op("vector", lambda e, bx: e.memset(o_raw[0:1, 2, :], 0.0), done=("init", 0))
        load_rows("wq", q_raw, wq)
        load_x(0)
        load("wk", WK[:, :, :], whole(wk))
        load("wk", WKI[:, :, :], whole(wki))
        load_ctx(0)
        load("wrest", IDENT[:, :], ident_h)
        for par in range(2):
            load("wrest", KS[KQ:TRK, par, :, :], sel_h)
        load("wv", v_raw if L0 else WV[:, :, :], whole(wv))
        load("wv", vi_raw if L0 else WVI[:, :, :], whole(wvi))
        load_rows("wrest", o_raw, wout)
        load("wrest", BIAS[:, :], bias)
        load("wrest", MASK[:, :], mask)
        if not L0:
            load("wrest", KMASK[:, :, :], kmask_h)
            load("wrest", VMASK[:, :], vmask_h)
        else:
            load("wrest", IPONE[:, :], vmask_h)

        def split_weight(pair_, n, raw, need, tag):
            hi, lo = pair_
            split_pair("wh", tag, (hi[0:n, :, :], lo[0:n, :, :]), raw[0:n, :, :], need, ("ws", tag), "vector")
        split_weight(WQ, CK, q_raw, [("wq", 0), ("init", 0)], 0)
        for c in range(3):
            split_xt(0, c)
        load_x(1)
        if L0:
            split_weight(WV, 128, v_raw, [("wv", 0)], 1)
            split_weight(WVI, 128, vi_raw, [("wv", 0)], 2)
        split_weight(WO, CK, o_raw, [("wrest", 0), ("init", 0)], 3)
        ms = lambda ap, v: op("vector", lambda e, bx: e.memset(ap, v), done=("init", 0))
        ms(VB[:, :, :, :, :], 0.0)
        if L0:
            ms(VA[:, :, :, :], 0.0)
            op("vector", lambda e, bx: e.memset(VA[:, :, :, D:D + 1], 1.0), need=[("init", 0)], done=("init", 0))
            ms(G0[:, :], 0.0)
            ms(CZ[0][:, :, :].bitcast(F32), 0.0)
            ms(CZ[1][:, :, :].bitcast(F32), 0.0)
            op("vector", lambda e, bx: e.tensor_copy(VB[:, :, 0, :, D], IPONE[:, :].unsqueeze(1).broadcast_to([128, 2, H])),
               need=[("wrest", 0), ("init", 0)], done=("init", 0))
            op("vector", lambda e, bx: e.memset(VB[:, :, 1, :, D:D + 1], 1.0), need=[("init", 0)], done=("init", 0))
        else:
            ms(KS[0:KQ, :, :, NT:T], 0.0)
            ms(GH[:, :, :, :].bitcast(F32), 0.0)
            ms(GL[:, :, :, :].bitcast(F32), 0.0)
            ms(E21[:, :], 0.0)
            ms(ONES[:, :], 1.0)
            ms(HALF[:, :, :], 0.5)
            ms(KBD[:, :, :, :], 0.0)
            op("vector", lambda e, bx: e.memset(E21[:, 21:22], 1.0), need=[("init", 0)], done=("init", 0))
            op("vector", lambda e, bx: e.memset(VB[:, :, 0, :, D:D + 1], 1.0), done=("init", 0))
            op("vector", lambda e, bx: e.memset(VB[0:NT - 128, :, 1, :, D:D + 1], 1.0), done=("init", 0))

    READY = [("wrest", 0), ("wv", 0), ("init", 0)]

    def load_x(b):
        for c, c0 in enumerate(CC):
            op("sync", lambda e, bx, c=c, c0=c0: e.dma_start(XT[0:CK, c, :], x_t[bx(b), c0:c0 + CK, :]),
               need=[("xts", b - 1)], done=(f"ldx{b % 2}", b), step=16)

    def load_ctx(b):
        op("sync", lambda e, bx: e.dma_start(CT[:, :, :], ctx_t[bx(b)].rearrange("(k q) t -> q k t", q=128)),
           need=[("cts", b - 1) if L0 else None, ("ctlast", b - 1), ("ctpool", b - 1)], done=(f"ldc{b % 2}", b), step=16)

    def load_residual(b):
        op("sync", lambda e, bx: e.dma_start(XB[:, :, :], x_nat[bx(b)].rearrange("(a q) c -> q a c", q=128)),
           need=[("y", (b - 1, 1))], done=(f"xn{b % 2}", b), step=16)

    def split_xt(b, c):
        split_pair("xth", (b, c), (XTS[0][0:CK, c, :], XTS[1][0:CK, c, :]), XT[0:CK, c, :],
                   [("ldx", b), ("qk", (b - 1, 2))], ("xts", b))

    def split_ctx(b):
        split_pair("cth", b, (CTS[0][:, :, :], CTS[1][:, :, :]), CT[:, :, :],
                   [("ldc", b), ("vlast", b - 1)], ("cts", b))

    def group(out, pairs, need, done=None):
        for n, (lhs, rhs) in enumerate(pairs):
            op("tensor", lambda e, bx, n=n, lhs=lhs, rhs=rhs: e.matmul(
                out, lhs, rhs, start=(n == 0), stop=(n == len(pairs) - 1)),
               need=need if n == 0 else (), done=done if n == len(pairs) - 1 else None)

    def group3(out, lhs, rhs, cut_l, cut_r, chunks, need, done=None):
        group(out, [(cut_l(lhs[i], c), cut_r(rhs[j], c)) for c in range(chunks) for i, j in ((0, 0), (1, 0), (0, 1))],
              need, done)

    def project_q(b, m):
        m0, mn = MT[m]
        qk_bank[m], last = misc()
        group3(MISC[qk_bank[m]][0:mn, 0:S], WQ, XTS, lambda w, c: w[0:CK, c, m0:m0 + mn], lambda x, c: x[0:CK, c, :], 3,
               [("ws", 0), ("xts", b), last])
        free_after(qk_bank[m], ("qkh", (b, m)))

    def project_k(b, m):
        (m0, mn), k = MT[m], qk_bank[m]
        group(MISC[k][0:mn, S:S + NT], [(WK[:, c, m0:m0 + mn], CT[:, c, 0:NT]) for c in range(KC)], [("wk", 0), ("ldc", b)])
        group(MISC[k][0:mn, S + NT:S + T], [(WKI[:, c, m0:m0 + mn], CT[:, c, NT:T]) for c in range(KC)],
              [("wk", 0), ("ldc", b)], ("qk", (b, m)))
        op("scalar", lambda e, bx: e.copy(QKF[0:mn, m, :], MISC[k][0:mn, :]),
           need=[("qk", (b, m)), ("parts", (b - 1, m)), ("qkfread", b - 1)], done=("qkf", (b, m)))
        op("scalar", lambda e, bx: e.copy(PARTS[0:mn, m, 0, :], MISC[k][0:mn, :]),
           need=[("spill", b - 1)], done=("qkh", (b, m)))
        op("gpsimd", lambda e, bx: e.tensor_tensor(RES[0:mn, :], QKF[0:mn, m, :], PARTS[0:mn, m, 0, :], ALU.subtract),
           need=[("qkh", (b, m)), ("parts", (b, m - 1) if m else (b - 1, 2))], done=("split", (b, m)))

    def split_rest(b, m):
        mn = MT[m][1]
        op("scalar", lambda e, bx: e.copy(PARTS[0:mn, m, 1, :], RES[0:mn, :]), need=[("split", (b, m))], done=("split2", (b, m)))
        op("gpsimd", lambda e, bx: e.tensor_tensor(PARTS[0:mn, m, 2, :], RES[0:mn, :], PARTS[0:mn, m, 1, :], ALU.subtract),
           need=[("split2", (b, m))], done=("parts", (b, m)))

    AHEAD = MT[0][1] // D

    def spill_parts(b, tiles=(0, 1, 2)):
        p = b % 2
        for m in tiles:
            m0, mn = MT[m]
            for qk in range(2):
                op("sync", lambda e, bx, m=m, m0=m0, mn=mn, qk=qk: e.dma_start(
                    parts_h[p, qk, :, m0:m0 + mn, :].rearrange("j r t -> r j t"),
                    PARTS[0:mn, m, :, qk * S:(qk + 1) * S]),
                   need=[("parts", (b, m)), ("stack", b - 2), ("ahead", b - 2) if b == 2 else None], done=("spill", b), step=16)

    def stack_parts(b, heads=slice(0, H)):
        p = b % 2
        kind = "ahead" if heads.stop < H else f"stack{p}"
        for r in range(len(Q_PARTS)):
            for qk, dst, parts, n in ((0, QS, Q_PARTS, S), (1, KS, K_PARTS, T if L0 else NT)):
                op("sync", lambda e, bx, r=r, qk=qk, dst=dst, parts=parts, n=n: e.dma_start(
                    dst[16 * r:16 * r + 16, p, heads, 0:n],
                    parts_h[p, qk, parts[r], D * heads.start:D * heads.stop, 0:n].rearrange("(h d) t -> d h t", d=D)),
                   need=[("spill", b), ("trans", 20 * (b - 2) + 19)],
                   done=(kind, b), step=16)

    def stacked(s):
        b, h = divmod(s, H)
        return [("ahead", 0)] if b == 0 and h < AHEAD else [("stack", b)]

    def project_v(b, which):
        p = b % 2
        k, last = misc()
        tag = ("vmm", (b, which))
        need = READY + [last] + ([("cts", b), ("ws", 1), ("ws", 2), ("cz", b)] if L0 else [("ldc", b)])
        if L0:
            src, t0, w, n, dst = {
                0: (CTS, 0, WV, NT, VA[:, p, :, 0:D]),
                1: (CZ, 0, WVI, 128, VB[:, p, 0, :, 0:D]),
                2: (CTS, 128, WVI, 128, VB[:, p, 1, :, 0:D]),
            }[which]
        else:
            src, t0, w, n, dst = {
                0: (CT, 0, WV, 128, VB[:, p, 0, :, 0:D]),
                1: (CT, 128, WV, NT - 128, VB[0:NT - 128, p, 1, :, 0:D]),
            }[which]
        tokens, features = (lambda x, c: x[:, c, t0:t0 + n]), (lambda y, c: y[:, c, :])
        if L0:
            group3(MISC[k][0:n, 0:C], src, w, tokens, features, KC, need, tag)
        else:
            group(MISC[k][0:n, 0:C], [(tokens(src, c), features(w, c)) for c in range(KC)], need, tag)
        src = MISC[k][0:n, 0:C].rearrange("p (h d) -> p h d", d=D)
        op("scalar", lambda e, bx: e.copy(dst, src), need=[tag, ("pv", (b - 2, 4))] + READY, done=("v", b))
        pl.at[("vs", (b, which))] = pl.at[("v", b)]
        free_after(k, ("vs", (b, which)))
        if which == (2 if L0 else 1):
            pl.at[("vlast" if L0 else "ctlast", b)] = pl.at[tag]

    def clear_text(b):
        op("scalar", lambda e, bx: e.copy(CZ[0][:, :, NT:128], CT[:, :, NT:128]),
           need=READY + [("ldc", b), ("vlast", b - 1)], done=("czh", b))
        op("gpsimd", lambda e, bx: e.tensor_tensor(CZ[1][:, :, NT:128], CT[:, :, NT:128], CZ[0][:, :, NT:128].bitcast(F32),
                                                   ALU.subtract),
           need=[("czh", b)], done=("cz", b))
        pl.at[("ctpool", b)] = pl.at[("cz", b)]

    def text_logits(b):
        k, last = misc()
        for a in range(2):
            group(MISC[k][:, a * NT:(a + 1) * NT],
                  [(QKF[0:mn, m, a * 128:(a + 1) * 128], QKF[0:mn, m, S:S + NT]) for m, (_, mn) in enumerate(MT)],
                  [("qkf", (b, 2)), last], ("tl", b))
        pl.at[("qkfread", b)] = pl.at[("tl", b)]
        lg = MISC[k][:, 0:2 * NT].rearrange("p (a t) -> p a t", a=2)
        op("vector", lambda e, bx: e.tensor_reduce(TPM[:, 0, :], lg, AX.X, ALU.max, negate=True),
           need=[("tl", b), ("tv", (b - 1, 3))], done=("tv", (b, 0)))
        op("vector", lambda e, bx: e.tensor_scalar(TPM[:, 1, :], TPM[:, 0, :], SCALE, None, ALU.mult),
           need=[("tv", (b, 0)), ("texp", b - 1)], done=("tv", (b, 1)))
        for a in range(2):
            op("scalar", lambda e, bx, a=a: e.activation(TP[:, a, :], MISC[k][:, a * NT:(a + 1) * NT], ACT.Exp,
                                                         bias=TPM[:, 1, a:a + 1], scale=SCALE,
                                                         accum_out=TPM[:, 2, a:a + 1]),
               need=[("tv", (b, 1)), ("tpt", b - 1)], done=("texp", b))
        free_after(k, ("texp", b))
        op("vector", lambda e, bx: e.reciprocal(TPM[:, 3, :], TPM[:, 2, :]), need=[("texp", b), ("tv", (b - 1, 3))], done=("tv", (b, 2)))
        op("vector", lambda e, bx: e.tensor_tensor(TP[:, :, :], TP[:, :, :],
                                                   TPM[:, 3, :].unsqueeze(2).broadcast_to([128, 2, NT]), ALU.mult),
           need=[("tv", (b, 2)), ("tpt", b - 1)], done=("tv", (b, 3)))

    def gram_text_ip(b):
        k, last = misc()
        group(MISC[k][0:NT, 0:NI], [(CT[:, c, 0:NT], CT[:, c, NT:T]) for c in range(KC)],
              READY + [("ldc", b), last], ("g0", b))
        pl.at[("ctlast", b)] = pl.at[("g0", b)]
        op("scalar", lambda e, bx: e.mul(G0[:, NT:T], MISC[k][0:NT, 0:NI], 0.5),
           need=[("g0", b), ("stmm", b - 1)] + READY, done=("g0s", b))
        free_after(k, ("g0s", b))

    def probs_t(b):
        k, last = misc()
        for a in range(2):
            op("tensor", lambda e, bx, a=a: e.transpose(MISC[k][0:NT, a * 128:(a + 1) * 128], TP[:, a, :], IDENT[:, :]),
               need=[("tv", (b, 3)), last], done=("tpt", b))
        op("scalar", lambda e, bx: e.copy(TPT[:, :], MISC[k][0:NT, 0:S]), need=[("tpt", b), ("stmm", b - 1)], done=("tpts", b))
        free_after(k, ("tpts", b))

    def sem_natural(b):
        k, last = misc()
        for a in range(2):
            group(MISC[k][:, a * NI:(a + 1) * NI], [(TPT[:, a * 128:(a + 1) * 128], G0[:, NT:T])],
                  [("tpts", b), ("g0s", b), last], ("snmm", b))
        op("scalar", lambda e, bx: e.copy(SN[:, b % 2, :, :], MISC[k][:, 0:2 * NI].rearrange("p (a t) -> p a t", a=2)),
           need=[("snmm", b), ("max", 20 * (b - 2) + 19)], done=("sn", b))
        free_after(k, ("sn", b))

    def sem_transposed(b):
        k, last = misc()
        for a in range(2):
            group(MISC[k][:, a * S:(a + 1) * S], [(G0[:, a * 128:(a + 1) * 128], TPT[:, :])], [last], ("stmm", b))
        op("scalar", lambda e, bx: e.copy(ST[:, b % 2, :], MISC[k][:, :]),
           need=[("stmm", b), ("sadd", 20 * (b - 2) + 19)], done=("st", b))
        free_after(k, ("st", b))

    def gram(b, which):
        p = b % 2
        k, last = misc()
        need = READY + [("ldc", b), last]
        if which == 0:
            group(MISC[k][:, 0:128], [(CT[:, c, 0:128], CT[:, c, 0:128]) for c in range(KC)], need)
            group(MISC[k][:, 128:132], [(CT[:, c, 0:128], CT[:, c, NT:T]) for c in range(KC)], (), ("gr", (b, 0)))
            jobs = [(0, slice(0, 128), MISC[k][:, 0:128])]
            n, c0, tt = 128, 128, 0
        else:
            n, c0, tt = NT - 128, NT, 1
            group(MISC[k][0:n, 0:T], [(CT[:, c, 128:NT], CT[:, c, :]) for c in range(KC)], need, ("gr", (b, 1)))
            jobs = [(1, slice(0, 128), MISC[k][0:n, 0:128]), (2, slice(0, n), MISC[k][0:n, 128:NT])]
        op("scalar", lambda e, bx: e.copy(VB[0:n, p, tt, :, D + 1:D + 5],
                                          MISC[k][0:n, c0:c0 + 4].unsqueeze(1).broadcast_to([n, H, 4])),
           need=[("gr", (b, which)), ("pv", (b - 2, 4))] + READY, done=("vc", b))
        for blk, cols, src in jobs:
            op("scalar", lambda e, bx, blk=blk, cols=cols, src=src: e.copy(GH[0:n, p, blk, cols], src),
               need=[("gpmm", 20 * (b - 2) + 19)], done=("gh", b))
        for blk, cols, src in jobs:
            op("vector", lambda e, bx, blk=blk, cols=cols, src=src: e.tensor_tensor(
                GL[0:n, p, blk, cols], src, GH[0:n, p, blk, cols].bitcast(F32), ALU.subtract),
               need=[("gh", b), ("gpmm", 20 * (b - 2) + 19)], done=("gl", b))
        pl.at[("gl", (b, which))] = pl.at[("gl", b)]
        free_after(k, ("gl", (b, which)))

    def gram_mirror(b):
        p, n = b % 2, NT - 128
        k, last = misc()
        op("tensor", lambda e, bx: e.transpose(MISC[k][:, 0:n], GH[0:n, p, 1, :].bitcast(F32), IDENT[0:n, 0:n]),
           need=[("gh", b), last], done=("g12", b))
        op("scalar", lambda e, bx: e.copy(GH[:, p, 3, 0:n], MISC[k][:, 0:n]),
           need=[("g12", b), ("gpmm", 20 * (b - 2) + 19)], done=("g12s", b))
        op("vector", lambda e, bx: e.tensor_scalar(GL[0:n, p, 1, :], GL[0:n, p, 1, :].bitcast(F32), 2.0, None, ALU.mult),
           need=[("gl", b)], done=("gl2", b))
        free_after(k, ("g12s", b))

    def ip_copies(b):
        ipc = CT[:, :, NT:T]
        op("gpsimd", lambda e, bx: e.tensor_tensor(SQ[:, :, :], ipc, ipc, ALU.mult),
           need=[("ldc", b), ("rnmm", b - 1)], done=("cip", b))
        op("gpsimd", lambda e, bx: e.tensor_copy(CIP[:, :, :].rearrange("p k (h n) -> p k h n", n=4),
                                                 ipc.unsqueeze(2).broadcast_to([128, KC, H, 4])),
           need=[("vipmm", b - 1)], done=("cip", b))
        pl.at[("ctpool", b)] = pl.at[("cip", b)]

    def ip_values(b):
        k, last = misc()
        group(MISC[k][0:80, 0:C], [(CIP[:, c, :], WVI[:, c, :]) for c in range(KC)], [("cip", b), last], ("vipmm", b))
        op("vector", lambda e, bx: e.tensor_tensor(VIP[:, b % 2, :], MISC[k][0:80, 0:C], VMASK[:, :], ALU.mult),
           need=READY + [("vipmm", b), ("ipmm", (b - 2, 1))], done=("vip", b))
        free_after(k, ("vip", b))

    def ip_norms(b):
        k, last = misc()
        group(MISC[k][:, 0:4], [(ONES[:, :], SQ[:, c, :]) for c in range(KC)], READY + [("cip", b), last], ("rnmm", b))
        op("vector", lambda e, bx: e.tensor_copy(RN[:, 0, :], MISC[k][:, 0:4]), need=[("rnmm", b), ("rn", (b - 1, 1))], done=("rn", (b, 0)))
        free_after(k, ("rn", (b, 0)))
        op("gpsimd", lambda e, bx: e.tensor_tensor(RN[:, 1, :], RN[:, 0, :], HALF[:, 0, 0:4], ALU.pow),
           need=READY + [("rn", (b, 0)), ("rn", (b - 1, 2))], done=("rn1", b))

    def invert_ip_norms(b):
        op("vector", lambda e, bx: e.tensor_scalar(RN[:, 2, :], RN[:, 1, :], EPS, None, ALU.max),
           need=[("rn1", b), ("rn", (b - 1, 2))], done=("rn", (b, 1)))
        op("vector", lambda e, bx: e.reciprocal(RNI[:, b % 2, :], RN[:, 2, :]), need=[("rn", (b, 1)), ("fu", (b - 2, 0))], done=("rn", (b, 2)))

    def ip_keys(b):
        op("vector", lambda e, bx: e.tensor_tensor(
            KBD[:, 0:2, :, :], KMASK[:, :, :].unsqueeze(1).broadcast_to([128, 2, 8, 4]),
            QKF[:, 0:2, S + NT:S + T].unsqueeze(2).broadcast_to([128, 2, 8, 4]), ALU.mult),
           need=READY + [("qkf", (b, 2)), ("scmm", b - 1)], done=("kbd", b))
        op("vector", lambda e, bx: e.tensor_tensor(
            KBD[0:64, 2, :, :], KMASK[0:64, :, :], QKF[0:64, 2, S + NT:S + T].unsqueeze(1).broadcast_to([64, 8, 4]),
            ALU.mult), done=("kbd", b))

    def ip_scores(b):
        k, last = misc()
        for a in range(2):
            for m, (_, mn) in enumerate(MT):
                w = mn // 4
                group(MISC[k][:, a * 80 + m * 32:a * 80 + m * 32 + w],
                      [(QKF[0:mn, m, a * 128:(a + 1) * 128], KBD[0:mn, m, 0:w // 4, :])],
                      [("kbd", b), last], ("scmm", b))
        pl.at[("qkfread", b)] = pl.at[("scmm", b)]
        op("vector", lambda e, bx: e.tensor_scalar(SC[:, b % 2, :, :], MISC[k][:, 0:160].rearrange("p (a n) -> p a n", a=2),
                                                   SCALE, None, ALU.mult),
           need=[("scmm", b), ("fu", (b - 2, 1))], done=("sc", b))
        free_after(k, ("sc", b))

    def maxima(s):
        b, h = divmod(s, H)
        p, k, gp, j = b % 2, s % 2, (s // HG) % 2, h % HG
        for a in range(2):
            op("tensor", lambda e, bx, a=a: e.matmul(
                NAT[k][:, a * T:(a + 1) * T], QS[0:KQ, p, h, a * 128:(a + 1) * 128], KS[0:KQ, p, h, :],
                start=True, stop=True),
               need=READY + stacked(s) + [("max", s - 2)], done=("nat", s))
        v = NAT[k][:, :].rearrange("p (a t) -> p a t", a=2)
        op("vector", lambda e, bx: e.tensor_reduce(MX[:, gp, :, j], v[:, :, 0:NT], AX.X, ALU.max),
           need=[("nat", s), ("mxt", s // HG - 2)] + ([("sn", b), ("max", s - 2)] if L0 else []),
           done=None if L0 else ("max", s))
        if L0:
            for a in range(2):
                op("vector", lambda e, bx, a=a: e.tensor_tensor_reduce(
                    TMP[:, k, a, :], v[:, a, NT:T], SN[:, p, a, :], 1.0, -3.0e38, ALU.add, ALU.max,
                    MX[:, gp, a, HG + j:HG + j + 1]), done=("max", s))

    def max_rows(g):
        b, hg = divmod(g, H // HG)
        gp, p = g % 2, b % 2
        w = 8 if L0 else 4
        if L0:
            k, last = misc()
            rows = MISC[k][0:w, 0:S]
        else:
            rows, last = PV[0:w, S:2 * S], ("nm", g - 1)
        for a in range(2):
            op("tensor", lambda e, bx, a=a: e.transpose(rows[:, a * 128:(a + 1) * 128], MX[:, gp, a, 0:w], IDENT[:, :]),
               need=[("max", HG * g + HG - 1), last, None if L0 else ("pvs", g - 4)], done=("mxt", g))
        op("scalar", lambda e, bx: e.mul(NH[0:w, gp, 0, :], rows, -1.0),
           need=[("mxt", g), ("mrow", g - 2)], done=("nh", g))
        nh_rows["last"] = rows, (k if L0 else None)

    def max_rows_low(g):
        b, hg = divmod(g, H // HG)
        gp, p = g % 2, b % 2
        w = 8 if L0 else 4
        rows, k = nh_rows["last"]
        op("vector", lambda e, bx: e.scalar_tensor_tensor(NH[0:w, gp, 1, :], rows, -1.0, NH[0:w, gp, 0, :],
                                                          ALU.mult, ALU.subtract),
           need=[("nh", g)], done=("nm", g))
        if L0:
            free_after(k, ("nm", g))
        for part in range(2):
            for grp in range(NG):
                r = KQ + NG * part + grp
                op("sync", lambda e, bx, part=part, grp=grp, r=r: e.dma_start(
                    QS[r:r + 1, p, HG * hg:HG * hg + HG, :], NH[HG * grp:HG * grp + HG, gp, part, :]),
                   need=READY + [("nm", g), ("trans", HG * (g - 10) + 3)], done=(f"mrow{gp}", g), step=16)

    nh_rows = {}

    def exponentials(s):
        b, h = divmod(s, H)
        p, k = b % 2, s % 2
        for a in range(2):
            op("tensor", lambda e, bx, a=a: e.matmul(
                TR[k][:, a * S:(a + 1) * S], KS[0:TRK, p, h, a * 128:(a + 1) * 128], QS[0:TRK, p, h, :],
                start=True, stop=True),
               need=READY + stacked(s) + [("mrow", s // HG), ("sadd" if L0 else "exp", s - 2)], done=("trans", s))
        if L0:
            op("vector", lambda e, bx: e.tensor_tensor(TA[:, k, :], TR[k][:, :], ST[:, p, :], ALU.add),
               need=[("trans", s), ("st", b), ("exp", s - 2)], done=("sadd", s))
        op("scalar", lambda e, bx: e.activation(P[:, s % NP, :], TA[:, k, :] if L0 else TR[k][:, :], ACT.Exp, scale=SCALE),
           need=[("sadd" if L0 else "trans", s), ("pv", divmod((s - NP) // HG, H // HG))],
           done=("exp", s))

    def split_exponentials(s):
        r, k = s % NP, s % NS
        op("scalar", lambda e, bx: e.copy(PH[:, k, :], P[:, r, :]), need=[("exp", s), ("gpmm", s - NS)], done=("ph", s))

    def multipliers(s):
        r, k = s % NP, s % NS
        op("vector", lambda e, bx: e.scalar_tensor_tensor(
            PM[:, k, :], P[:, r, :], 2.0, PH[:, k, :].bitcast(F32), ALU.mult, ALU.subtract),
           need=[("ph", s), ("zp", s - NS)], done=("pm", s))

    def quadratic(s):
        b, h = divmod(s, H)
        p, k = b % 2, s % NS
        n2 = NT - 128
        p0, p1 = PH[:, k, 0:S], PH[0:n2, k, S:2 * S]
        group(GP[:, 0:S], [(GH[:, p, 0, :], p0), (GL[:, p, 0, :], p0), (GH[0:n2, p, 1, :], p1), (GL[0:n2, p, 1, :], p1)],
              [("gl2", b), ("g12s", b),
               ("ph", s), ("zp", s - 1)])
        group(GP[:, S:2 * S], [(GH[:, p, 3, :], p0), (GH[0:n2, p, 2, :], p1), (GL[0:n2, p, 2, :], p1)], (), ("gpmm", s))
        op("vector", lambda e, bx: e.tensor_tensor(ZP[:, s % 2, :], GP[:, :], PM[:, k, :], ALU.mult),
           need=[("gpmm", s), ("pm", s), ("zs", s - 2)], done=("zp", s))
        op("gpsimd", lambda e, bx: e.tensor_tensor(ZS[:, s % NP, :], ZP[:, s % 2, 0:S], ZP[:, s % 2, S:2 * S], ALU.add),
           need=[("zp", s), ("pv", divmod((s - NP) // HG, H // HG))], done=("zs", s))

    def weighted_sums(g):
        b, hg = divmod(g, H // HG)
        p = b % 2
        lab = ("pv", (b, hg))
        need = [("exp", HG * g + HG - 1), ("v", b), ("pvs", g - 1)]
        if not L0:
            need.append(("nm", min(g + 3, B * H // HG - 1)))
        rounds = []
        if L0:
            rounds.append([(PV[SLOT * j:SLOT * (j + 1), 0:S], VA[:, p, HG * hg + j, :], P[0:NT, (HG * g + j) % NP, 0:S], True, True)
                           for j in range(HG)])
            for tt in range(2):
                rounds.append([(PV[SLOT * j:SLOT * (j + 1), S:2 * S], VB[:, p, tt, HG * hg + j, :],
                                P[:, (HG * g + j) % NP, tt * S:(tt + 1) * S], tt == 0, tt == 1) for j in range(HG)])
        else:
            need.append(("vc", b))
            need.append(("zs", HG * g + HG - 1))
            for tt in range(2):
                rounds.append([(PV[SLOT * j:SLOT * (j + 1), 0:S], VB[:, p, tt, HG * hg + j, :],
                                P[:, (HG * g + j) % NP, tt * S:(tt + 1) * S], tt == 0, False) for j in range(HG)])
            rounds.append([(PV[SLOT * j:SLOT * (j + 1), 0:S], E21[:, :], ZS[:, (HG * g + j) % NP, :], False, True)
                           for j in range(HG)])
        flat = [x for r in rounds for x in r]
        for n, (out, lhs, rhs, st, sp) in enumerate(flat):
            op("tensor", lambda e, bx, out=out, lhs=lhs, rhs=rhs, st=st, sp=sp: e.matmul(out, lhs, rhs, start=st, stop=sp),
               need=need if n == 0 else (), done=lab if n == len(flat) - 1 else None)
        w = 2 * S if L0 else S
        op("scalar", lambda e, bx: e.copy(PVS[:, 0:w], PV[:, 0:w]), need=[lab, ("ont", g - 1)], done=("pvs", g))

    def to_natural(g):
        b, hg = divmod(g, H // HG)
        k, last = misc()
        n = 4 if L0 else 2
        for a in range(n):
            op("tensor", lambda e, bx, a=a: e.transpose(MISC[k][:, a * 128:(a + 1) * 128], PVS[:, a * 128:(a + 1) * 128], IDENT[:, :]),
               need=[("pvs", g), last], done=("ont", g))
        op("scalar", lambda e, bx: e.copy(
            ON[:, b % 2, :, :, :].rearrange("p v a (h s) -> p (v a) h s", s=NV)[:, :, HG * hg:HG * hg + HG, :],
            MISC[k][:, 0:n * 128].rearrange("p (v h s) -> p v h s", v=n, s=SLOT)[:, :, :, 0:NV]),
           need=[("ont", g), ("hs", b - 2)], done=("on", g))
        free_after(k, ("on", g))

    def on_view(b, v):
        return ON[:, b % 2, v, :, :].rearrange("p a (h s) -> p a h s", s=NV)

    def residual(b):
        op("gpsimd", lambda e, bx: e.tensor_tensor(XB[:, :, :], XB[:, :, :],
                                                   BIAS[:, :].unsqueeze(1).broadcast_to([128, 2, C]), ALU.add),
           need=READY + [("xn", b)], done=("xb", b))

    HSV = HS[:, :, :].rearrange("p a (h d) -> p a h d", d=D)

    def combine_l0(b):
        A_, B_ = on_view(b, 0), on_view(b, 1)
        g = 5 * b + 4
        op("vector", lambda e, bx: e.reciprocal(R1[:, 0, :, :], A_[:, :, :, D]), need=[("on", g), ("hs", b - 1)], done=("cmb", (b, 0)))
        op("vector", lambda e, bx: e.reciprocal(R1[:, 1, :, :], B_[:, :, :, D]), done=("cmb", (b, 1)))
        for a in range(2):
            op("vector", lambda e, bx, a=a: e.tensor_scalar(R1[:, 1, a, :], R1[:, 1, a, :], MASK[:, a:a + 1], None, ALU.mult),
               need=READY + [("cmb", (b, 1))], done=("cmb", (b, 2)))
        bc = lambda v: R1[:, v, :, :].unsqueeze(3).broadcast_to([128, 2, H, D])
        for v, X in enumerate((A_, B_)):
            op("gpsimd", lambda e, bx, v=v, X=X: e.tensor_tensor(X[:, :, :, 0:D], X[:, :, :, 0:D], bc(v), ALU.mult),
               need=[("cmb", (b, 2))], done=("cmb", (b, 3)))
        op("gpsimd", lambda e, bx: e.tensor_tensor(HSV, A_[:, :, :, 0:D], B_[:, :, :, 0:D], ALU.add),
           need=[("cmb", (b, 3)), ("hst", (b - 1, 1))], done=("hs", b))

    def combine_l1(b, stage):
        A_ = on_view(b, 0)
        g = 5 * b + 4
        V = lambda fn, need=(), done=None: op("vector", fn, need=need, done=done) if stage == now[0] else None
        q = b % 2
        now = [0]
        rz = R1[:, 0, :, :]
        V(lambda e, bx: e.reciprocal(rz, A_[:, :, :, D]), [("on", g), ("hs", b - 1), ("fu", (b - 1, 0))], ("cmb", (b, 0)))
        V(lambda e, bx: e.tensor_scalar(NRM[:, 0, :, :], A_[:, :, :, D + 5], 0.0, None, ALU.max), [("nrm", b - 1)], ("cmb", (b, 1)))
        if stage == 0:
            op("gpsimd", lambda e, bx: e.tensor_tensor(NRM[:, 1, :, :], NRM[:, 0, :, :], HALF[:, :, :], ALU.pow),
               need=READY + [("cmb", (b, 1)), ("cmb", (b - 1, 2))], done=("nrm", b))
        now[0] = 1
        V(lambda e, bx: e.tensor_tensor(NRM[:, 2, :, :], NRM[:, 1, :, :], rz, ALU.mult), [("nrm", b), ("cmb", (b - 1, 3))], ("cmb", (b, 2)))
        V(lambda e, bx: e.tensor_scalar(NRM[:, 2, :, :], NRM[:, 2, :, :], EPS, None, ALU.max), [("cmb", (b, 2))], ("cmb", (b, 3)))
        V(lambda e, bx: e.reciprocal(NRM[:, 3, :, :], NRM[:, 2, :, :]), [("cmb", (b, 3)), ("cmb", (b - 1, 5))], ("cmb", (b, 4)))
        V(lambda e, bx: e.scalar_tensor_tensor(NRM[:, 3, :, :], NRM[:, 3, :, :], 0.5, rz, ALU.mult, ALU.mult), [("cmb", (b, 4))], ("cmb", (b, 5)))
        F = lambda i: FU[:, i, :, :].rearrange("p a (h n) -> p a h n", n=4)
        V(lambda e, bx: e.tensor_tensor(F(0), A_[:, :, :, D + 1:D + 5], NRM[:, 3, :, :].unsqueeze(3).broadcast_to([128, 2, H, 4]), ALU.mult),
          [("cmb", (b, 5)), ("fu", (b - 1, 0))], ("fu", (b, 5)))
        V(lambda e, bx: e.tensor_tensor(FU[:, 1, :, :].rearrange("p a (h n) -> p (a h) n", n=4),
                                        FU[:, 0, :, :].rearrange("p a (h n) -> p (a h) n", n=4),
                                        RNI[:, q, :].unsqueeze(1).broadcast_to([128, 2 * H, 4]), ALU.mult),
          [("fu", (b, 5)), ("rn", (b, 2)), ("fu", (b - 1, 1))], ("fu", (b, 0)))
        V(lambda e, bx: e.tensor_tensor(FU[:, 2, :, :], FU[:, 1, :, :], SC[:, q, :, :], ALU.add), [("fu", (b, 0)), ("sc", b), ("fu", (b - 1, 2))], ("fu", (b, 1)))
        V(lambda e, bx: e.tensor_reduce(FM[:, 0, :, :], F(2), AX.X, ALU.max), [("fu", (b, 1)), ("fu", (b - 1, 2))], ("fu", (b, 6)))
        V(lambda e, bx: e.tensor_tensor(F(3), F(2), FM[:, 0, :, :].unsqueeze(3).broadcast_to([128, 2, H, 4]), ALU.subtract),
          [("fu", (b, 6)), ("fexp", b - 1)], ("fu", (b, 2)))
        if stage == 1:
            op("scalar", lambda e, bx: e.activation(FU[:, 4, :, :], FU[:, 3, :, :], ACT.Exp), need=[("fu", (b, 2)), ("fu", (b - 1, 4))], done=("fexp", b))
        now[0] = 2
        V(lambda e, bx: e.tensor_reduce(FM[:, 1, :, :], F(4), AX.X, ALU.add), [("fexp", b), ("fu", (b - 1, 3))], ("fu", (b, 7)))
        V(lambda e, bx: e.reciprocal(FM[:, 2, :, :], FM[:, 1, :, :]), [("fu", (b, 7)), ("fu", (b - 1, 3))], ("fu", (b, 8)))
        for a in range(2):
            V(lambda e, bx, a=a: e.tensor_scalar(FM[:, 3, a, :], FM[:, 2, a, :], MASK[:, a:a + 1], None, ALU.mult),
              READY + [("fu", (b, 8)), ("fu", (b - 1, 4))], ("fu", (b, 3)))
        V(lambda e, bx: e.tensor_tensor(F(5), F(4), FM[:, 3, :, :].unsqueeze(3).broadcast_to([128, 2, H, 4]), ALU.mult),
          [("fu", (b, 3)), ("ptt", b - 1)], ("fu", (b, 4)))
        V(lambda e, bx: e.tensor_tensor(HSV, A_[:, :, :, 0:D], rz.unsqueeze(3).broadcast_to([128, 2, H, D]), ALU.mult),
          [("hst", (b - 1, 1))], ("tx", b))

    def ip_probs_t(b):
        k, last = misc()
        for a in range(2):
            op("tensor", lambda e, bx, a=a: e.transpose(MISC[k][0:80, a * 128:(a + 1) * 128], FU[:, 5, a, :], IDENT[:, :]),
               need=[("fu", (b, 4)), last], done=("ptt", b))
        op("scalar", lambda e, bx: e.copy(PT[:, :], MISC[k][0:80, 0:S]), need=[("ptt", b), ("ipmm", (b - 1, 1))], done=("pt", b))
        free_after(k, ("pt", b))

    def ip_out(b, a):
        k, last = misc()
        group(MISC[k][:, 0:C], [(PT[:, a * 128:(a + 1) * 128], VIP[:, b % 2, :])], [("pt", b), ("vip", b), last], ("ipmm", (b, a)))
        op("vector", lambda e, bx: e.tensor_tensor(HS[:, a, :], HS[:, a, :], MISC[k][:, 0:C], ALU.add),
           need=[("ipmm", (b, a)), ("tx", b)], done=("hs", b))
        pl.at[("hsa", (b, a))] = pl.at[("hs", b)]
        free_after(k, ("hsa", (b, a)))

    def hs_t(b, a):
        k, last = misc()
        for c, c0 in enumerate(CC):
            op("tensor", lambda e, bx, c=c, c0=c0: e.transpose(MISC[k][0:CK, c * 128:(c + 1) * 128], HS[:, a, c0:c0 + CK], IDENT[:, :]),
               need=[("hs", b), last], done=("hst", (b, a)))
        src = MISC[k][0:CK, 0:384].rearrange("p (c q) -> p c q", c=3)
        hi, lo = (t[0:CK, :, a * 128:(a + 1) * 128] for t in HT)
        op("scalar", lambda e, bx: e.copy(hi, src), need=[("hst", (b, a)), ("omm", (b - 1, 1))], done=("hth", (b, a)))
        op("vector", lambda e, bx: e.tensor_tensor(lo, src, hi.bitcast(F32), ALU.subtract),
           need=[("hth", (b, a)), ("omm", (b - 1, 1))], done=("ht", (b, a)))
        free_after(k, ("ht", (b, a)))

    def project_out(b, a):
        k, last = misc()
        group3(MISC[k][:, 0:C], HT, WO, lambda x, c: x[0:CK, c, a * 128:(a + 1) * 128], lambda w, c: w[0:CK, c, :], 3,
               [("ht", (b, a)), ("ws", 3), last], ("omm", (b, a)))
        op("vector", lambda e, bx: e.tensor_tensor(Y[:, a, :], MISC[k][:, 0:C], XB[:, a, :], ALU.add),
           need=[("omm", (b, a)), ("xb", b), ("store", b - 1)] + ([("ytt", (b - 1, 1))] if L0 else []), done=("y", (b, a)))
        free_after(k, ("y", (b, a)))
        if a == 1:
            op("sync", lambda e, bx: e.dma_start(y_nat[bx(b)].rearrange("(a q) c -> q a c", q=128), Y[:, :, :]),
               need=[("y", (b, 1))], done=("store", b), step=16)

    def y_transposed(b, a):
        k, last = misc()
        for c, c0 in enumerate(CC):
            op("tensor", lambda e, bx, c=c, c0=c0: e.transpose(MISC[k][0:CK, c * 128:(c + 1) * 128], Y[:, a, c0:c0 + CK], IDENT[:, :]),
               need=[("y", (b, a)), last], done=("ytt", (b, a)))
        op("scalar", lambda e, bx: e.copy(YT[0:CK, :, a * 128:(a + 1) * 128], MISC[k][0:CK, 0:384].rearrange("p (c q) -> p c q", c=3)),
           need=[("ytt", (b, a)), ("storet", b - 1)], done=("yt", (b, a)))
        free_after(k, ("yt", (b, a)))
        if a == 1:
            for c, c0 in enumerate(CC):
                skip = c // 2
                op("sync", lambda e, bx, c=c, c0=c0 + skip, skip=skip: e.dma_start(
                    y_t[bx(b), c0:c0 + CK - skip, :], YT[skip:CK, c, :]),
                   need=[("yt", (b, 1))], done=("storet", b), step=16)

    agenda = {}

    def at(slot, fn, *args):
        agenda.setdefault(slot, []).append((fn, args))

    for b in range(B):
        base = H * (b - 1)
        if b > 1:
            at(base - (17 if L0 else 19), load_x, b)
        if b:
            at(base - (16 if L0 else 11), load_ctx, b)
            for c in range(3):
                at(base + c - (11 if L0 else 16), split_xt, b, c)
        if L0:
            at(base + 1, split_ctx, b)
        for m, (q, k) in enumerate(((-6, -5), (-4, -2), (-1, 0)) if L0 else ((-10, -8), (-4, -3), (-2, 0))):
            at(base + q, project_q, b, m)
            at(base + k, project_k, b, m)
            at(base + k + 1, split_rest, b, m)
            if b == 0:
                at(base + k + 1, spill_parts, b, (m,))
                if m != 1:
                    at(base + k + 1, stack_parts, b, slice(AHEAD, H) if m else slice(0, AHEAD))
        if b:
            at(base + 1, spill_parts, b)
            at(base + 2, stack_parts, b)
        if L0:
            at(base, clear_text, b)
            at(base + 2, text_logits, b)
            at(base + 3, gram_text_ip, b)
            at(base + 4, project_v, b, 0)
            at(base + 5, probs_t, b)
            at(base + 7, sem_natural, b)
            at(base + 7, sem_transposed, b)
            at(base + 8, project_v, b, 1)
            at(base + 10, project_v, b, 2)
        else:
            at(base - 5, ip_copies, b)
            at(base + 4, gram, b, 0)
            at(base + 5, gram, b, 1)
            at(base + 6, project_v, b, 0)
            at(base + 7, gram_mirror, b)
            at(base + 8, project_v, b, 1)
            at(base + 8, ip_keys, b)
            at(base + 8, ip_norms, b)
            at(base + 11, invert_ip_norms, b)
            at(base + 11, ip_scores, b)
            at(base + 14, ip_values, b)
        base = H * b
        for s in range(base, base + H):
            at(s - LEAD, maxima, s)
            at(s, exponentials, s)
            if not L0:
                at(s, split_exponentials, s)
                at(s + 1, multipliers, s)
                at(s + 2, quadratic, s)
        for hg in range(H // HG):
            g = b * (H // HG) + hg
            at(HG * g + HG - LEAD + 1, max_rows, g)
            at(HG * g + HG - LEAD + 1, max_rows_low, g)
            at(HG * g + HG + (1 if L0 else 3), weighted_sums, g)
            at(HG * g + HG + (3 if L0 else 5), to_natural, g)
        base += H
        at(base + (-3 if L0 else 4), load_residual, b)
        at(base + (1 if L0 else 10), residual, b)
        if L0:
            at(base + 4, combine_l0, b)
            at(base + 8, hs_t, b, 0)
            at(base + 8, hs_t, b, 1)
            at(base + 11, project_out, b, 0)
            at(base + 12, project_out, b, 1)
            at(base + 14, y_transposed, b, 0)
            at(base + 15, y_transposed, b, 1)
        else:
            at(base + 7, combine_l1, b, 0)
            at(base + 10, combine_l1, b, 1)
            at(base + 11, combine_l1, b, 2)
            at(base + 13, ip_probs_t, b)
            at(base + 14, ip_out, b, 0)
            at(base + 14, ip_out, b, 1)
            at(base + 15, hs_t, b, 0)
            at(base + 15, hs_t, b, 1)
            at(base + 21, project_out, b, 0)
            at(base + 22, project_out, b, 1)

    setup()
    rank = {maxima: 0, max_rows: 1, exponentials: 2, split_exponentials: 2, multipliers: 3.2, quadratic: 3, weighted_sums: 4, to_natural: 5, project_k: 4.5, max_rows_low: 3.5}
    for slot in sorted(agenda):
        if slot >= 0 and slot % (2 * H) == 0:
            pl.start(slot // (2 * H))
        for fn, args in sorted(agenda[slot], key=lambda x: rank.get(x[0], 6)):
            fn(*args)
    assert misc_state["n"] // B * 2 % n_misc == 0 and 2 * H % NP == 0
    pl.emit(nc, ctx, gate)


def build(nc, a, out):
    x1 = nc.dram_tensor("x1", (B, S, C), F32, kind="Internal").ap()
    x1_t = nc.dram_tensor("x1_t", (B, C, S), F32, kind="Internal").ap()
    parts = nc.dram_tensor("qk_parts", (2, 2, 3, C, S), BF16, kind="Internal").ap()
    with ExitStack() as gates:
        gate = {k: gates.enter_context(nc.semaphore("s_gate_" + k)) for k in ("sync", "gpsimd")}
        with ExitStack() as ctx:
            xattn_layer(nc, ctx, gate, True, a["x"], a["x_t"], a["ctx_t"], a["mask"],
                        a["L0_xattn_Wq"], a["L0_xattn_Wk"], a["L0_xattn_Wv"], a["L0_xattn_Wk_ip"], a["L0_xattn_Wv_ip"],
                        a["L0_xattn_Wout"], a["bias0"], a["ident"], a["sel0"], None, a["ip_rows"], parts, x1, x1_t)
        with ExitStack() as ctx:
            xattn_layer(nc, ctx, gate, False, x1, x1_t, a["ctx_t"], a["mask"],
                        a["L1_xattn_W_q"], a["L1_xattn_W_k"], a["L1_xattn_W_v"], a["L1_xattn_W_k_ip"], a["L1_xattn_W_v_ip"],
                        a["L1_xattn_W_out"], a["bias1"], a["ident"], a["sel1"], a["kmask"], a["vmask"], parts, out, None)


def kernel(**inputs):
    import numpy as np
    import ml_dtypes
    import concourse.bacc as _bacc
    from concourse.bass_utils import run_bass_kernel_spmd as _run

    arr = {k: np.ascontiguousarray(v) for k, v in inputs.items()}
    ctx2048 = arr.pop("ctx_2048")
    arr["x_t"] = np.ascontiguousarray(arr["x"].transpose(0, 2, 1))
    arr["ctx_t"] = np.ascontiguousarray(ctx2048.transpose(0, 2, 1))
    arr["bias0"] = np.ascontiguousarray(np.broadcast_to(arr.pop("L0_xattn_bout"), (128, C)))
    arr["bias1"] = np.ascontiguousarray(np.broadcast_to(arr.pop("L1_xattn_b_out"), (128, C)))
    arr["ident"] = np.eye(128, dtype=np.float32)
    for n, nt in ((0, 77), (1, T - 4)):
        s = np.zeros((2, 2 - n, H, T), np.float32)
        s[:, 0, :, :nt] = 1
        if n == 0:
            s[:, 1, :, nt:] = 1
        arr[f"sel{n}"] = s.reshape(-1, H, T).astype(ml_dtypes.bfloat16)
    arr["ip_rows"] = np.repeat((np.arange(128) >= 77).astype(np.float32)[:, None], H, axis=1)
    arr["mask"] = np.ascontiguousarray(arr.pop("fside_S_0").reshape(2, 128).T)
    arr["kmask"] = np.ascontiguousarray(np.repeat((np.arange(128)[:, None] // D == np.arange(8)[None, :])
                                                  .astype(np.float32)[:, :, None], 4, axis=2))
    arr["vmask"] = (np.arange(80)[:, None] // 4 == np.arange(C)[None, :] // D).astype(np.float32)

    nc = _bacc.Bacc("TRN2", target_bir_lowering=False, num_devices=1)
    arrays, args = {}, {}
    for name, v in arr.items():
        arrays[f"in_{name}"] = v
        args[name] = nc.dram_tensor(f"in_{name}", v.shape, mybir.dt.from_np(v.dtype), kind="ExternalInput").ap()
    out = nc.dram_tensor("out_0", (B, S, C), F32, kind="ExternalOutput").ap()
    build(nc, args, out)
    r = _run(nc, [arrays], core_ids=[0])
    return r.results[0]["out_0"]
```
